# Optimizing a Trainium2 kernel written in Bass

```python
import numpy as np
import jax
import jax.numpy as jnp

def _softmax(x, axis=-1):
    return jax.nn.softmax(x, axis=axis)

def _gelu(x):
    return jax.nn.gelu(x, approximate=True)

def _silu(x):
    return jax.nn.silu(x)

def _sigmoid(x):
    return jax.nn.sigmoid(x)

def _layernorm(x, axis=-1, eps=1e-05):
    m = jnp.mean(x, axis=axis, keepdims=True)
    v = jnp.var(x, axis=axis, keepdims=True)
    return (x - m) / jnp.sqrt(v + eps)

def _scatter_add(tgt, idx, src, axis=0):
    return tgt.at[idx].add(src)

def _segment_sum(src, seg, n):
    return jax.ops.segment_sum(src, seg, n)
kernel_name = 'mk_xattn_ffn_d2_seqx_r8_52f7ee'

def setup_inputs(seed: int=0):
    np.random.seed(seed)
    _w = jnp.asarray

    def _rec_inputs():
        import jax
        import jax.numpy as jnp
        _rk = jax.random.key(seed)
        x = -0.0002928 + 1 * jax.random.normal(jax.random.fold_in(_rk, 1), (8, 256, 128), jnp.float32)
        _lenS = 256 - jax.random.randint(jax.random.fold_in(_rk, 7), (8,), 0, max(1, 256 // 4) + 1, jnp.int32)
        _lenS2 = 256 - jax.random.randint(jax.random.fold_in(_rk, 8), (8,), 0, max(1, 256 // 4) + 1, jnp.int32)
        _ctx_1024P = jax.random.normal(jax.random.fold_in(_rk, 11), (8, 16, 128), jnp.float32)
        _ctx_1024c = jax.random.dirichlet(jax.random.fold_in(_rk, 511), 0.3 * jnp.ones((16,), jnp.float32), (8, 256))
        _ctx_1024t = jnp.einsum('bsk,bkd->bsd', _ctx_1024c, _ctx_1024P)
        _ctx_1024t = _ctx_1024t * jax.lax.rsqrt(jnp.mean(jnp.square(_ctx_1024t)) + 1e-12) * 0.953939
        ctx_1024 = -1.39393e-06 + 0.999914 * (_ctx_1024t + 0.3 * jax.random.normal(jax.random.fold_in(_rk, 611), (8, 256, 128), jnp.float32))
        _validS = jnp.arange(256)[None, :] < _lenS[:, None]
        _validS2 = jnp.arange(256)[None, :] < _lenS2[:, None]
        _causal = jnp.tril(jnp.ones((256, 256), dtype=bool))
        mask_Bx1xSxS2_ik1 = jnp.where(jnp.broadcast_to(_validS2[:, None, None, :], (8, 1, 256, 256)), 1, 0).astype(jnp.int32)
        return (x, ctx_1024, mask_Bx1xSxS2_ik1)
    x, ctx_1024, mask_Bx1xSxS2_ik1 = _rec_inputs()

    def _L0_xattn_setup():
        import jax, jax.numpy as jnp
        import numpy as np
        D_MODEL = 128
        HEADS = 16
        HEAD_DIM = D_MODEL // HEADS
        key = jax.random.key(seed)
        ks = jax.random.split(key, 11)
        B, S = (2, 256)
        scale = 1.0 / np.sqrt(D_MODEL)
        inp = {'Q': jax.random.normal(ks[0], (B, S, D_MODEL), jnp.float32), 'K': jax.random.normal(ks[1], (B, S, D_MODEL), jnp.float32), 'V': jax.random.normal(ks[2], (B, S, D_MODEL), jnp.float32), 'Wq': jax.random.normal(ks[3], (D_MODEL, D_MODEL), jnp.float32) * scale, 'bq': jnp.zeros((D_MODEL,), jnp.float32), 'Wk': jax.random.normal(ks[4], (D_MODEL, D_MODEL), jnp.float32) * scale, 'bk': jnp.zeros((D_MODEL,), jnp.float32), 'Wv': jax.random.normal(ks[5], (D_MODEL, D_MODEL), jnp.float32) * scale, 'bv': jnp.zeros((D_MODEL,), jnp.float32), 'Wo': jax.random.normal(ks[6], (D_MODEL, D_MODEL), jnp.float32) * scale, 'bo': jnp.zeros((D_MODEL,), jnp.float32)}
        return inp
    _L0_xattn_all = _L0_xattn_setup()
    _L0_xattn_in = {k: v for k, v in _L0_xattn_all.items() if k in ('Wq', 'bq', 'Wk', 'bk', 'Wv', 'bv', 'Wo', 'bo')}
    del _L0_xattn_all

    def _L0_ffn_setup():
        import jax, jax.numpy as jnp
        import numpy as np
        B, S, D_MODEL, D_HIDDEN = (4, 256, 128, 512)

        def act_quant(x):
            scale = 127.0 / jnp.clip(jnp.max(jnp.abs(x), axis=-1, keepdims=True), 1e-05)
            return jnp.clip(jnp.round(x * scale), -128, 127) / scale

        def weight_quant(w):
            scale = 1.0 / jnp.clip(jnp.mean(jnp.abs(w)), 1e-05)
            return jnp.clip(jnp.round(w * scale), -1, 1) / scale

        def bit_linear(x, w):
            xq = x + jax.lax.stop_gradient(act_quant(x) - x)
            wq = w + jax.lax.stop_gradient(weight_quant(w) - w)
            return jnp.einsum('bsd,hd->bsh', xq, wq)

        def depthwise_conv1d(x_bcl, w, b):
            y = jax.lax.conv_general_dilated(x_bcl, w, window_strides=(1,), padding=[(1, 1)], dimension_numbers=('NCH', 'OIH', 'NCH'), feature_group_count=x_bcl.shape[1])
            return y + b[None, :, None]
        key = jax.random.key(seed)
        ks = jax.random.split(key, 5)
        lim1 = 1.0 / np.sqrt(D_MODEL)
        lim2 = 1.0 / np.sqrt(D_HIDDEN)
        limc = 1.0 / np.sqrt(3.0)
        return {'x': jax.random.normal(ks[0], (B, S, D_MODEL), dtype=jnp.float32), 'w1': jax.random.uniform(ks[1], (D_HIDDEN, D_MODEL), jnp.float32, -lim1, lim1), 'conv_w': jax.random.uniform(ks[2], (D_HIDDEN, 1, 3), jnp.float32, -limc, limc), 'conv_b': jax.random.uniform(ks[3], (D_HIDDEN,), jnp.float32, -limc, limc), 'w2': jax.random.uniform(ks[4], (D_MODEL, D_HIDDEN), jnp.float32, -lim2, lim2)}
    _L0_ffn_all = _L0_ffn_setup()
    _L0_ffn_in = {k: v for k, v in _L0_ffn_all.items() if k in ('w1', 'conv_w', 'conv_b', 'w2')}
    del _L0_ffn_all

    def _L1_xattn_setup():
        import jax, jax.numpy as jnp
        import numpy as np
        NUM_HEADS = 16
        D_MODEL = 128
        DEPTH = D_MODEL // NUM_HEADS

        def _split_heads(x):
            B, S, _ = x.shape
            return x.reshape(B, S, NUM_HEADS, DEPTH).transpose(0, 2, 1, 3)
        key = jax.random.key(seed)
        ks = jax.random.split(key, 12)
        B, S = (4, 256)
        q = jax.random.normal(ks[0], (B, S, D_MODEL), dtype=jnp.float32)
        k = jax.random.normal(ks[1], (B, S, D_MODEL), dtype=jnp.float32)
        v = jax.random.normal(ks[2], (B, S, D_MODEL), dtype=jnp.float32)
        mask = jax.random.randint(ks[3], (B, 1, S, S), 0, 2, dtype=jnp.int32)
        sc = 1.0 / np.sqrt(D_MODEL)
        Wq = jax.random.normal(ks[4], (D_MODEL, D_MODEL), dtype=jnp.float32) * sc
        Wk = jax.random.normal(ks[5], (D_MODEL, D_MODEL), dtype=jnp.float32) * sc
        Wv = jax.random.normal(ks[6], (D_MODEL, D_MODEL), dtype=jnp.float32) * sc
        Wo = jax.random.normal(ks[7], (D_MODEL, D_MODEL), dtype=jnp.float32) * sc
        bq = jnp.zeros((D_MODEL,), jnp.float32)
        bk = jnp.zeros((D_MODEL,), jnp.float32)
        bv = jnp.zeros((D_MODEL,), jnp.float32)
        bo = jnp.zeros((D_MODEL,), jnp.float32)
        return {'query': q, 'key': k, 'value': v, 'mask': mask, 'Wq': Wq, 'bq': bq, 'Wk': Wk, 'bk': bk, 'Wv': Wv, 'bv': bv, 'Wo': Wo, 'bo': bo}
    _L1_xattn_all = _L1_xattn_setup()
    _L1_xattn_in = {k: v for k, v in _L1_xattn_all.items() if k in ('Wq', 'bq', 'Wk', 'bk', 'Wv', 'bv', 'Wo', 'bo')}
    del _L1_xattn_all

    def _L1_ffn_setup():
        import jax, jax.numpy as jnp
        import numpy as np
        H = 128
        EH = 512
        E = 8
        TOP_K = 2
        EPS = 1e-09
        key = jax.random.key(seed)
        k1, k2, k3, k4 = jax.random.split(key, 4)
        s_h = 1.0 / np.sqrt(H)
        s_eh = 1.0 / np.sqrt(EH)
        return {'hidden_states': jax.random.normal(k1, (4, 256, H), dtype=jnp.float32), 'router_w': jax.random.uniform(k2, (E, H), jnp.float32, -s_h, s_h), 'fc1_w': jax.random.uniform(k3, (E, EH, H), jnp.float32, -s_h, s_h), 'fc2_w': jax.random.uniform(k4, (E, H, EH), jnp.float32, -s_eh, s_eh)}
    _L1_ffn_all = _L1_ffn_setup()
    _L1_ffn_in = {k: v for k, v in _L1_ffn_all.items() if k in ('router_w', 'fc1_w', 'fc2_w')}
    del _L1_ffn_all
    return {'x': x, 'ctx_1024': ctx_1024, 'mask_Bx1xSxS2_ik1': mask_Bx1xSxS2_ik1, 'L0_xattn_Wq': _L0_xattn_in['Wq'], 'L0_xattn_bq': _L0_xattn_in['bq'], 'L0_xattn_Wk': _L0_xattn_in['Wk'], 'L0_xattn_bk': _L0_xattn_in['bk'], 'L0_xattn_Wv': _L0_xattn_in['Wv'], 'L0_xattn_bv': _L0_xattn_in['bv'], 'L0_xattn_Wo': _L0_xattn_in['Wo'], 'L0_xattn_bo': _L0_xattn_in['bo'], 'L0_ffn_w1': _L0_ffn_in['w1'], 'L0_ffn_conv_w': _L0_ffn_in['conv_w'], 'L0_ffn_conv_b': _L0_ffn_in['conv_b'], 'L0_ffn_w2': _L0_ffn_in['w2'], 'L1_xattn_Wq': _L1_xattn_in['Wq'], 'L1_xattn_bq': _L1_xattn_in['bq'], 'L1_xattn_Wk': _L1_xattn_in['Wk'], 'L1_xattn_bk': _L1_xattn_in['bk'], 'L1_xattn_Wv': _L1_xattn_in['Wv'], 'L1_xattn_bv': _L1_xattn_in['bv'], 'L1_xattn_Wo': _L1_xattn_in['Wo'], 'L1_xattn_bo': _L1_xattn_in['bo'], 'L1_ffn_router_w': _L1_ffn_in['router_w'], 'L1_ffn_fc1_w': _L1_ffn_in['fc1_w'], 'L1_ffn_fc2_w': _L1_ffn_in['fc2_w']}

def reference(x, ctx_1024, mask_Bx1xSxS2_ik1, L0_xattn_Wq, L0_xattn_bq, L0_xattn_Wk, L0_xattn_bk, L0_xattn_Wv, L0_xattn_bv, L0_xattn_Wo, L0_xattn_bo, L0_ffn_w1, L0_ffn_conv_w, L0_ffn_conv_b, L0_ffn_w2, L1_xattn_Wq, L1_xattn_bq, L1_xattn_Wk, L1_xattn_bk, L1_xattn_Wv, L1_xattn_bv, L1_xattn_Wo, L1_xattn_bo, L1_ffn_router_w, L1_ffn_fc1_w, L1_ffn_fc2_w):
    import jax
    import jax.numpy as jnp

    def _L0_xattn_ref(Q, K, V, Wq, bq, Wk, bk, Wv, bv, Wo, bo):
        import jax, jax.numpy as jnp
        import numpy as np
        D_MODEL = 128
        HEADS = 16
        HEAD_DIM = D_MODEL // HEADS
        B, S, _ = Q.shape

        def proj(x, W, b):
            y = x @ W.T + b
            return y.reshape(B, S, HEADS, HEAD_DIM).transpose(0, 2, 1, 3)
        q = proj(Q, Wq, bq)
        k = proj(K, Wk, bk)
        v = proj(V, Wv, bv)
        scores = jnp.einsum('bhqd,bhkd->bhqk', q, k) / jnp.sqrt(jnp.asarray(HEAD_DIM, q.dtype))
        weights = jax.nn.softmax(scores, axis=-1)
        ctx = jnp.einsum('bhqk,bhkd->bhqd', weights, v)
        concat = ctx.transpose(0, 2, 1, 3).reshape(B, S, D_MODEL)
        return concat @ Wo.T + bo

    def _L0_ffn_ref(x, w1, conv_w, conv_b, w2):
        import jax, jax.numpy as jnp
        import numpy as np
        B, S, D_MODEL, D_HIDDEN = (4, 256, 128, 512)

        def act_quant(x):
            scale = 127.0 / jnp.clip(jnp.max(jnp.abs(x), axis=-1, keepdims=True), 1e-05)
            return jnp.clip(jnp.round(x * scale), -128, 127) / scale

        def weight_quant(w):
            scale = 1.0 / jnp.clip(jnp.mean(jnp.abs(w)), 1e-05)
            return jnp.clip(jnp.round(w * scale), -1, 1) / scale

        def bit_linear(x, w):
            xq = x + jax.lax.stop_gradient(act_quant(x) - x)
            wq = w + jax.lax.stop_gradient(weight_quant(w) - w)
            return jnp.einsum('bsd,hd->bsh', xq, wq)

        def depthwise_conv1d(x_bcl, w, b):
            y = jax.lax.conv_general_dilated(x_bcl, w, window_strides=(1,), padding=[(1, 1)], dimension_numbers=('NCH', 'OIH', 'NCH'), feature_group_count=x_bcl.shape[1])
            return y + b[None, :, None]
        h = bit_linear(x, w1)
        h = depthwise_conv1d(h.transpose(0, 2, 1), conv_w, conv_b)
        h = h.transpose(0, 2, 1)
        h = jax.nn.silu(h)
        return bit_linear(h, w2)

    def _L1_xattn_ref(query, key, value, mask, Wq, bq, Wk, bk, Wv, bv, Wo, bo):
        import jax, jax.numpy as jnp
        import numpy as np
        NUM_HEADS = 16
        D_MODEL = 128
        DEPTH = D_MODEL // NUM_HEADS

        def _split_heads(x):
            B, S, _ = x.shape
            return x.reshape(B, S, NUM_HEADS, DEPTH).transpose(0, 2, 1, 3)
        B, Sq, _ = query.shape
        q = _split_heads(query @ Wq + bq)
        k = _split_heads(key @ Wk + bk)
        v = _split_heads(value @ Wv + bv)
        scale = 1.0 / jnp.sqrt(jnp.asarray(DEPTH, q.dtype))
        logits = jnp.einsum('bhqd,bhkd->bhqk', q, k) * scale
        logits = logits + mask.astype(logits.dtype) * -1000000000.0
        attn = jax.nn.softmax(logits, axis=-1)
        out = jnp.einsum('bhqk,bhkd->bhqd', attn, v)
        out = out.transpose(0, 2, 1, 3).reshape(B, Sq, D_MODEL)
        return out @ Wo + bo

    def _L1_ffn_ref(hidden_states, router_w, fc1_w, fc2_w):
        import jax, jax.numpy as jnp
        import numpy as np
        H = 128
        EH = 512
        E = 8
        TOP_K = 2
        EPS = 1e-09
        orig_shape = hidden_states.shape
        flat = hidden_states.reshape(-1, H)
        gate_logits = flat @ router_w.T
        gate_probs = jax.nn.softmax(gate_logits, axis=-1)
        topk_w, topk_idx = jax.lax.top_k(gate_probs, TOP_K)
        topk_w = topk_w / jnp.maximum(topk_w.sum(-1, keepdims=True), EPS)
        w_te = jnp.einsum('tke,tk->te', jax.nn.one_hot(topk_idx, E, dtype=topk_w.dtype), topk_w)
        out = jnp.zeros_like(flat)
        for e in range(E):
            h = jax.nn.silu(flat @ fc1_w[e].T)
            y = h @ fc2_w[e].T
            out = out + w_te[:, e:e + 1] * y
        return out.reshape(orig_shape)
    x = x + _L0_xattn_ref(_layernorm(x, axis=-1), ctx_1024, ctx_1024, L0_xattn_Wq, L0_xattn_bq, L0_xattn_Wk, L0_xattn_bk, L0_xattn_Wv, L0_xattn_bv, L0_xattn_Wo, L0_xattn_bo)
    x = x + _L0_ffn_ref(_layernorm(x, axis=-1), L0_ffn_w1, L0_ffn_conv_w, L0_ffn_conv_b, L0_ffn_w2)
    x = x + _L1_xattn_ref(_layernorm(x, axis=-1), ctx_1024, ctx_1024, mask_Bx1xSxS2_ik1, L1_xattn_Wq, L1_xattn_bq, L1_xattn_Wk, L1_xattn_bk, L1_xattn_Wv, L1_xattn_bv, L1_xattn_Wo, L1_xattn_bo)
    x = x + _L1_ffn_ref(_layernorm(x, axis=-1), L1_ffn_router_w, L1_ffn_fc1_w, L1_ffn_fc2_w)
    return x

_drawn_inputs = setup_inputs


def setup_inputs(seed=0):
    import zlib

    import numpy as np

    out = dict(_drawn_inputs(seed))
    spreads = {'L0_xattn_bq': (0.0, 0.372),
     'L0_xattn_bk': (0.0, 0.8),
     'L0_xattn_bv': (0.0, 0.1),
     'L0_xattn_bo': (0.0, 0.1),
     'L1_xattn_bq': (0.0, 0.294),
     'L1_xattn_bk': (0.0, 0.8),
     'L1_xattn_bv': (0.0, 0.1),
     'L1_xattn_bo': (0.0, 0.1)}
    factors = {}
    for name, (base, spread) in spreads.items():
        noise = np.random.default_rng([zlib.crc32(name.encode()), seed]).standard_normal(out[name].shape)
        drawn = base * np.exp(spread * noise) if base else spread * noise
        out[name] = jnp.asarray(drawn.astype(out[name].dtype))
    for name, factor in factors.items():
        out[name] = (out[name] * factor).astype(out[name].dtype)
    return out
```

```python
import numpy as np
import concourse.bass as bass
from concourse import mybir
from contextlib import ExitStack

F32 = mybir.dt.float32
F32R = mybir.dt.float32r
BF16 = mybir.dt.bfloat16
I32 = mybir.dt.int32
U32 = mybir.dt.uint32
ALU = mybir.AluOpType
ACT = mybir.ActivationFunctionType
AX = mybir.AxisListType

P = 128
DMA = 16
LN_EPS = 1e-5
QUANT_EPS = 1e-5
ROUND = 1.5 * 2.0 ** 23
MASK_A, MASK_B = 625.0 * 512.0, 3125.0
assert MASK_A * MASK_B == 1e9


def build(nc, inp, out, stages=4):
    NB, S, D = inp["x"].shape
    NT = S // P
    H = 16
    DH = D // H
    SETS, HPS = 4, 4
    HR = P // HPS
    FF = inp["L0_ffn_w1"].shape[0]
    FC = FF // P
    E, EH, _ = inp["L1_ffn_fc1_w"].shape
    EC = EH // P
    GT = 4
    NG = NB * NT // GT
    QSCALE = float(1.0 / np.sqrt(np.float32(DH)))
    assert D == P and DH * H == D and SETS * HPS == H

    with ExitStack() as ctx:
        def sb(name, shape, dt=F32):
            return ctx.enter_context(nc.sbuf_tensor(name, shape, dt))

        def sem(name):
            return ctx.enter_context(nc.semaphore(name))

        ps = ctx.enter_context(nc.psum_tensor("ps", [P, 8, 512], F32))
        BANK_S = (0, 1)
        BANK_T = (2, 3, 4)
        BANK_O = (5, 6)
        BANK_M = 7

        ident = sb("ident", [P, P])
        ident_bf = sb("ident_bf", [P, P], BF16)
        neg_mask_eye = sb("neg_mask_eye", [P, P], F32R)
        mean_ones = sb("mean_ones", [P, P])
        minus_half = sb("minus_half", [P, NT])
        zeros = sb("zeros", [P, S])
        iota_e = sb("iota_e", [P, E])

        x_res = sb("x_res", [P, NB * NT, D])
        xnT_all = sb("xnT_all", [P, NB, S])
        xhT_all = sb("xhT_all", [P, NB, S], F32R)
        xlT_all = sb("xlT_all", [P, NB, S], F32R)
        w_te = sb("w_te", [P, NB * NT, E])

        w_raw = sb("w_raw", [P, 8, D])
        wq, wk, wv, wo, bq, bk, bv, bo = ([None, None] for _ in range(8))
        for l in range(2):
            wq[l], wk[l], wv[l], wo[l] = (sb(f"w{n}{l}", [P, D]) for n in "qkvo")
            bq[l], bk[l] = (sb(f"b{n}{l}", [P, 1]) for n in "qk")
            bv[l], bo[l] = (sb(f"b{n}{l}", [P, D]) for n in "vo")
        ffn_raw = sb("ffn_raw", [P, 2, FC, P])
        w1T = sb("w1T", [P, FC, P])
        w2T = sb("w2T", [P, FC, D], BF16)
        conv_w = sb("conv_w", [P, FC, 3])
        conv_b = sb("conv_b", [P, FC])
        wq_stat = sb("wq_stat", [P, 8])
        router_raw = sb("router_raw", [E, D])
        routerT = sb("routerT", [P, E])
        fc_raw = sb("fc_raw", [P, 2, 2, EC * P])
        fc1_hi = sb("fc1_hi", [P, E, EC, P], F32R)
        fc1_lo = sb("fc1_lo", [P, E, EC, P], F32R)
        fc2T = sb("fc2T", [P, E, EC, D])

        q_stack = [sb(f"q_stack{r}", [P, SETS, S], F32R) for r in range(2)]
        k_blocks = [sb(f"k_blocks{r}", [P, SETS, HPS, S], F32R) for r in range(2)]
        v_aug = [sb(f"v_aug{r}", [P, NT, H, HR]) for r in range(2)]
        ctx_in = sb("ctx_in", [P, NT, D])
        ctxT = sb("ctxT", [P, S])
        qk_hi = sb("qk_hi", [P, 2, S], F32R)
        qk_lo = sb("qk_lo", [P, 2, S], F32R)
        neg_max = sb("neg_max", [P, NT, H])
        max_split = sb("max_split", [P, NT, 2, SETS // 2, 2, HPS], F32R)
        maxT = sb("maxT", [SETS * HPS, 2, S])
        probs = sb("probs", [P, 2, HPS, NT, S])
        o_raw = sb("o_raw", [P, SETS, S])
        rden = sb("rden", [P, NT, H])
        o_norm = sb("o_norm", [P, NT, D])
        o_normT = sb("o_normT", [P, S])
        mask_in = sb("mask_in", [P, NT, S], I32)
        mask_q = [sb(f"mask_q{r}", [P, NT, S], F32R) for r in range(2)]
        mask_k = [sb(f"mask_k{r}", [P, NT, S], F32R) for r in range(2)]

        ln_st = sb("ln_st", [P, NT, 6])
        ln_mv = sb("ln_mv", [P, NT, 2])
        ln_ve = sb("ln_ve", [P, NT])
        ln_rstd = sb("ln_rstd", [P, NT])
        xn = sb("xn", [P, NT, D])
        qa = sb("qa", [P, NT, 3])
        r_x = sb("r_x", [P, S])
        r_nmax = sb("r_nmax", [P, NT])
        r_e = sb("r_e", [P, NT, E])
        r_sum = sb("r_sum", [P, NT])
        r_top = sb("r_top", [P, NT, 8])
        r_idx = sb("r_idx", [P, NT, 8], U32)
        r_idf = sb("r_idf", [P, NT, 2])
        r_den = sb("r_den", [P, NT])
        r_w = sb("r_w", [P, NT, 2])
        r_pick = sb("r_pick", [P, 2, NT, E])

        def in_fc2T(k):
            return fc2T[:, 2 * k:2 * k + 2, :, :].rearrange("p e c d -> p (e c d)")

        f_conv = in_fc2T(0).rearrange("p (c t) -> p c t", c=FC)
        f_act = in_fc2T(1).rearrange("p (c t) -> p c t", c=FC)
        f_round = in_fc2T(2).rearrange("p (i h) -> p i h", i=NT)
        f_int = sb("f_int", [P, NT, FF], BF16)
        f_intT = sb("f_intT", [P, NT, FC, P], BF16)
        fa = sb("fa", [P, NT, 4])

        hT = probs[:, :, :, :, :].rearrange("p r c k q -> p r c (k q)")

        q_dram = [nc.dram_tensor(f"q_dram{r}", (H, 4, DH, S), F32).ap() for r in range(2)]
        k_dram = [nc.dram_tensor(f"k_dram{r}", (H, 3, DH, S), F32).ap() for r in range(2)]

        held = sem("held")
        x_loaded = sem("x_loaded")
        w_loaded = sem("w_loaded")
        ffn_loaded = sem("ffn_loaded")
        bias_loaded = sem("bias_loaded")
        fc_loaded = [sem("fc_loaded0"), sem("fc_loaded1")]
        zero_stored = sem("zero_stored")
        out_stored = sem("out_stored")
        const_ready = sem("const_ready")
        cast_ready = sem("cast_ready")
        stack_zeroed = sem("stack_zeroed")
        wT_ps, wT_sb = sem("wT_ps"), sem("wT_sb")
        f_stat, f_mean, f_tern = sem("f_stat"), sem("f_mean"), sem("f_tern")
        f_wT_ps, f_wT_sb = sem("f_wT_ps"), sem("f_wT_sb")
        fc_ps, fc_hi, fc_done = sem("fc_ps"), sem("fc_hi"), sem("fc_done")

        class Ln:
            def __init__(self, n):
                self.st = sem(n + "_ln_stats")
                self.mv = sem(n + "_ln_mean_var")
                self.ve = sem(n + "_ln_var_eps")
                self.rstd = sem(n + "_ln_rstd")
                self.xn = sem(n + "_ln_xn")
                self.q = sem(n + "_ln_quant")
                self.xT = sem(n + "_ln_xT")
                self.xs = sem(n + "_ln_xT_sb")

        class Att:
            def __init__(self, n):
                s = lambda x: sem(n + "_" + x)
                self.ctx_in, self.cT_ps, self.cT_sb = s("ctx_in"), s("ctxT_ps"), s("ctxT_sb")
                self.qk_ps, self.qk_hi, self.qk_lo = s("qk_ps"), s("qk_hi"), s("qk_lo")
                self.to_dram = s("to_dram")
                self.stack = [s("stack_half0"), s("stack_half1")]
                self.v_ps, self.v_sb = s("v_ps"), s("v_sb")
                self.s_ps, self.s_max = s("s_ps"), s("s_max")
                self.m_hi, self.m_split = s("m_hi"), s("m_split")
                self.mT_ps, self.mT_sb = s("mT_ps"), s("mT_sb")
                self.m_in = [s("m_in_half0"), s("m_in_half1")]
                self.t_ps, self.p_sb = s("t_ps"), s("p_sb")
                self.pv = s("pv")
                self.o_sb = s("o_sb")
                self.oT_ps, self.rden, self.o_norm = s("oT_ps"), s("rden"), s("o_norm")
                self.nT_ps, self.nT_sb = s("nT_ps"), s("nT_sb")
                self.y_ps, self.x_new = s("y_ps"), s("x_new")
                self.k_in, self.k_q = s("mask_in"), s("mask_q")
                self.kT_ps, self.kT_sb = s("maskT_ps"), s("maskT_sb")
                self.r_ps, self.r = s("router_ps"), s("router")
                self.r_x, self.r_exp = s("router_x"), s("router_exp")
                self.x_hi = s("x_hi")

        ln_pre, ln_a0, ln_f0, ln_a1 = Ln("pre"), Ln("a0"), Ln("f0"), Ln("a1")
        att = [Att("a0"), Att("a1")]
        h_ps, h_tap, h_conv, h_act = sem("h_ps"), sem("h_tap"), sem("h_conv"), sem("h_act")
        g_ps, g_stat, g_round, g_int = sem("g_ps"), sem("g_stat"), sem("g_round"), sem("g_int")
        gi_ps, gi_sb, fy_ps, fx_new = sem("gi_ps"), sem("gi_sb"), sem("fy_ps"), sem("fx_new")
        fc1_ps, h_sb, y_ps, y_used = sem("fc1_ps"), sem("h_sb"), sem("y_ps"), sem("y_used")

        block = ctx.enter_context(nc.Block())

        def exists(b):
            return not isinstance(b, int) or 0 <= b < NB

        def after(b, k):
            return not isinstance(b, int) or b > k

        def bodies(eng, body):
            for b in range(-2, 2):
                body(b, b % 2)
            with eng.Fori(1, NB // 2 - 1) as t:
                body(t * 2, 0)
                body(t * 2 + 1, 1)
            for b in range(NB - 2, NB + 1):
                body(b, b % 2)

        def batches(eng, step, end=NB):
            step(0)
            with eng.Fori(1, end) as b:
                step(b)

        def one(t, b):
            return t[:, bass.ds(b, 1)].rearrange("p o f -> p (o f)")

        def x_tiles(b):
            return x_res[:, bass.ds(b * NT, NT), :]

        def x_tile(b, i):
            return x_res[:, bass.ds(b * NT + i, 1), :].rearrange("p o d -> p (o d)")

        def hold(eng, semaphore, value):
            eng.wait_ge(semaphore, value)
            eng.sem_inc(held, 1)

        def ln_stats(eng, s, b, produced):
            hold(eng, *produced)
            for i in range(NT):
                last = eng.bn_stats(ln_st[:, i, :], x_tile(b, i))
            last.then_inc(s.st, 1)
            hold(eng, s.st, b + 1)
            for i in range(NT):
                last = eng.bn_aggr(ln_mv[:, i, :], ln_st[:, i, :])
            last.then_inc(s.mv, 1)

        def ln_power(eng, s, b):
            hold(eng, s.mv, b + 1)
            eng.tensor_scalar(ln_ve[:, :], ln_mv[:, :, 1], LN_EPS, None, ALU.add).then_inc(s.ve, 1)
            eng.wait_ge(s.ve, b + 1)
            eng.tensor_tensor(ln_rstd[:, :], ln_ve[:, :], minus_half[:, :], ALU.pow).then_inc(s.rstd, 1)

        def ln_apply(eng, s, b, add_bias=None):
            eng.wait_ge(s.rstd, b + 1)
            eng.wait_ge(s.xT, b)
            for i in range(NT):
                last = eng.tensor_scalar(xn[:, i, :], x_tile(b, i), ln_mv[:, i, 0:1], ln_rstd[:, i:i + 1],
                                         ALU.subtract, ALU.mult)
            last.then_inc(s.xn, 1)
            if add_bias is not None:
                eng.wait_ge(s.xn, b + 1)
                eng.tensor_tensor(x_tiles(b), x_tiles(b),
                                  add_bias[:, None, :].to_broadcast([P, NT, D]), ALU.add).then_inc(s.q, 1)

        def quantise_rows(eng, s, b):
            eng.wait_ge(s.xn, b + 1)
            eng.tensor_reduce(qa[:, :, 0], xn[:, :, :], AX.X, ALU.max, apply_absolute_value=True).then_inc(s.q, 1)
            eng.wait_ge(s.q, b * 6 + 1)
            eng.tensor_scalar(qa[:, :, 0], qa[:, :, 0], QUANT_EPS, None, ALU.max).then_inc(s.q, 1)
            eng.wait_ge(s.q, b * 6 + 2)
            eng.reciprocal(qa[:, :, 1], qa[:, :, 0])
            eng.tensor_scalar(qa[:, :, 2], qa[:, :, 0], 1.0 / 127.0, None, ALU.mult).then_inc(s.q, 1)
            eng.wait_ge(s.q, b * 6 + 3)
            eng.tensor_scalar(qa[:, :, 1], qa[:, :, 1], 127.0, None, ALU.mult).then_inc(s.q, 1)
            eng.wait_ge(s.q, b * 6 + 4)
            for i in range(NT):
                last = eng.tensor_scalar(xn[:, i, :], xn[:, i, :], qa[:, i, 1:2], ROUND, ALU.mult, ALU.add)
            last.then_inc(s.q, 1)
            eng.wait_ge(s.q, b * 6 + 5)
            for i in range(NT):
                eng.tensor_scalar(xn[:, i, :], xn[:, i, :], ROUND + 127.0, ROUND - 128.0, ALU.min, ALU.max)
            eng.drain()
            for i in range(NT):
                last = eng.tensor_scalar(xn[:, i, :], xn[:, i, :], ROUND, qa[:, i, 2:3], ALU.subtract, ALU.mult)
            last.then_inc(s.q, 1)

        def xn_transposes(eng, s, b, bank, col, ready):
            eng.wait_ge(*ready)
            for i in range(NT):
                last = eng.transpose(ps[:, bank, col + i * P:col + (i + 1) * P], xn[:, i, :], ident[:, :])
            last.then_inc(s.xT, 1)

        def stack_loads(eng, a, b, r, half):
            sets = slice(2 * half, 2 * half + 2)
            for j in range(HPS):
                q_src = q_dram[r].rearrange("(s j) t d q -> j (t d) s q", j=HPS)[j]
                k_src = k_dram[r].rearrange("(s j) t d q -> j (t d) s q", j=HPS)[j]
                eng.dma_start(q_stack[r][j * HR:(j + 1) * HR, sets, :].bitcast(F32),
                              q_src[:, sets, :]).then_inc(a.stack[half], DMA)
                eng.dma_start(k_blocks[r][j * HR + DH:(j + 1) * HR, sets, j, :].bitcast(F32),
                              k_src[:, sets, :]).then_inc(a.stack[half], DMA)

        def max_loads(eng, a, b, r, half):
            eng.wait_ge(a.mT_sb, b * 2 + half + 1)
            for s in range(2):
                for part in range(2):
                    row = (s * 2 + part) * HPS
                    eng.dma_start(q_stack[r][part:part + (HPS - 1) * HR + 1:HR, 2 * half + s, :].bitcast(F32),
                                  maxT[row:row + HPS, half, :]).then_inc(a.m_in[half], DMA)

        def attention_sync(eng, l):
            a = att[l]
            c_src = inp["ctx_1024"]

            def body(b, r):
                if exists(b + 2):
                    eng.wait_ge(a.cT_ps, b + 2)
                    eng.dma_start(ctx_in[:, :, :], c_src[bass.ds(b + 2, 1)].rearrange("o (i p) d -> p (o i) d", p=P)
                                  ).then_inc(a.ctx_in, DMA)
                    if l == 1:
                        eng.wait_ge(a.k_q, b + 2)
                        m_src = inp["mask_Bx1xSxS2_ik1"][bass.ds(b + 2, 1)]
                        eng.dma_start(mask_in[:, :, :], m_src.rearrange("o u (i p) k -> p (o u i) k", p=P)
                                      ).then_inc(a.k_in, DMA)
                if exists(b):
                    max_loads(eng, a, b, r, 1)
                if exists(b + 2):
                    eng.wait_ge(a.qk_lo, b + 3)
                    if after(b, -1):
                        for half in range(2):
                            eng.wait_ge(a.stack[half], (b + 1) * 8 * DMA)
                    elif l == 1:
                        for half in range(2):
                            eng.wait_ge(att[0].stack[half], NB * 8 * DMA)
                    for t, part in ((1, qk_hi), (2, qk_hi), (3, qk_lo)):
                        eng.dma_start(q_dram[r][:, t], part[:, 0, :].bitcast(F32)).then_inc(a.to_dram, DMA)
                    for t, part in ((0, qk_hi), (1, qk_lo), (2, qk_hi)):
                        eng.dma_start(k_dram[r][:, t], part[:, 1, :].bitcast(F32)).then_inc(a.to_dram, DMA)
                    eng.wait_ge(a.to_dram, (b + 3) * 6 * DMA)
                    if exists(b):
                        eng.wait_ge(a.t_ps, b * 16 + 8)
                    else:
                        if l == 0:
                            eng.wait_ge(stack_zeroed, 2)
                            eng.wait_ge(zero_stored, 2 * DMA)
                        else:
                            eng.wait_ge(att[0].t_ps, NB * 16)
                    stack_loads(eng, a, b + 2, r, 0)
                if exists(b + 1):
                    max_loads(eng, a, b + 1, 1 - r, 0)
                if exists(b + 2):
                    if exists(b):
                        eng.wait_ge(a.t_ps, b * 16 + 16)
                    stack_loads(eng, a, b + 2, r, 1)

            bodies(eng, body)

        @block.sync
        def _(eng):
            eng.dma_start(x_res[:, :, :], inp["x"].rearrange("b (i p) d -> p (b i) d", p=P)).then_inc(x_loaded, DMA)
            for l in range(2):
                for n, w in enumerate("qkvo"):
                    dst = w_raw[:, n, :] if l == 0 else (w_raw[:, 4, :] if w == "q" else (wk, wv, wo)["kvo".index(w)][1][:, :])
                    eng.dma_start(dst, inp[f"L{l}_xattn_W{w}"]).then_inc(w_loaded, DMA)
            for l in range(2):
                eng.dma_start(bq[l][:, :], inp[f"L{l}_xattn_bq"].rearrange("(p o) -> p o", o=1)).then_inc(bias_loaded, DMA)
                eng.dma_start(bk[l][:, :], inp[f"L{l}_xattn_bk"].rearrange("(p o) -> p o", o=1)).then_inc(bias_loaded, DMA)
                eng.dma_start(bv[l][:, :], inp[f"L{l}_xattn_bv"].partition_broadcast(P)).then_inc(bias_loaded, DMA)
                eng.dma_start(bo[l][:, :], inp[f"L{l}_xattn_bo"].partition_broadcast(P)).then_inc(bias_loaded, DMA)
            eng.wait_ge(const_ready, 2)
            for r in range(2):
                for h0 in range(0, H, H):
                    eng.dma_start(q_dram[r][:, 0], zeros[:, :]).then_inc(zero_stored, DMA)
            eng.dma_start(ffn_raw[:, 0, :, :], inp["L0_ffn_w1"].rearrange("(c p) d -> p c d", p=P)).then_inc(ffn_loaded, DMA)
            eng.dma_start(ffn_raw[:, 1, :, :], inp["L0_ffn_w2"].rearrange("d (c p) -> d c p", p=P)).then_inc(ffn_loaded, DMA)
            eng.dma_start(conv_w[:, :, :], inp["L0_ffn_conv_w"].rearrange("(c p) o k -> p (c o) k", p=P)).then_inc(ffn_loaded, DMA)
            eng.dma_start(conv_b[:, :], inp["L0_ffn_conv_b"].rearrange("(c p) -> p c", p=P),
                          allow_slow_non_contiguous=True).then_inc(ffn_loaded, DMA)
            eng.dma_start(router_raw[:, :], inp["L1_ffn_router_w"]).then_inc(ffn_loaded, DMA)
            attention_sync(eng, 0)
            if stages >= 3:
                attention_sync(eng, 1)
            if stages >= 4:
                for e in range(E):
                    if e >= 2:
                        eng.wait_ge(fc_ps, (e - 1) * 2)
                    eng.dma_start(fc_raw[:, e % 2, 0, :].rearrange("p (c d) -> p c d", c=EC),
                                  inp["L1_ffn_fc1_w"][e].rearrange("(c p) d -> p c d", p=P)).then_inc(fc_loaded[e % 2], DMA)
                    eng.dma_start(fc_raw[:, e % 2, 1, :], inp["L1_ffn_fc2_w"][e]).then_inc(fc_loaded[e % 2], DMA)
                with eng.Fori(0, NG) as g:
                    eng.wait_ge(y_used, (g * E + E + 2))
                    dst = out.rearrange("b (i p) d -> p (b i) d", p=P)
                    eng.dma_start(dst[:, bass.ds(g * GT, GT), :], x_res[:, bass.ds(g * GT, GT), :]).then_inc(out_stored, DMA)
                eng.wait_ge(out_stored, NG * DMA)
            else:
                if stages == 1:
                    eng.wait_ge(ln_a0.xn, NB)
                elif stages == 2:
                    eng.wait_ge(ln_f0.xn, NB)
                    eng.wait_ge(ln_f0.q, NB)
                else:
                    eng.wait_ge(att[1].x_new, NB)
                eng.dma_start(out.rearrange("b (i p) d -> p (b i) d", p=P), x_res[:, :, :]).then_inc(out_stored, DMA)
                eng.wait_ge(out_stored, DMA)

        @block.gpsimd
        def _(eng):
            eng.memset(ident[:, :], 0.0).then_inc(const_ready, 1)
            eng.memset(zeros[:, :], 0.0).then_inc(const_ready, 1)
            eng.wait_ge(const_ready, 1)
            eng.affine_select(out=ident[:, :], in_=ident[:, :], compare_op=ALU.not_equal, fill=1.0, base=0,
                              pattern=[[-1, P]], channel_multiplier=1).then_inc(const_ready, 1)
            eng.memset(minus_half[:, :], -0.5).then_inc(const_ready, 1)
            eng.memset(mean_ones[:, :], 1.0 / (FF * D)).then_inc(const_ready, 1)
            for e in range(E):
                last = eng.memset(iota_e[:, e:e + 1], float(e))
            last.then_inc(const_ready, 1)
            for r in range(2):
                eng.memset(v_aug[r][:, :, :, :], 1.0).then_inc(const_ready, 1)

            def powers(s):
                with eng.Fori(0, NB) as b:
                    ln_power(eng, s, b)

            eng.wait_ge(const_ready, 8)
            powers(ln_pre)
            powers(ln_a0)
            if stages >= 2:
                powers(ln_f0)
            if stages >= 3:
                powers(ln_a1)

        def attention_scalar(eng, l):
            a = att[l]

            def body(b, r):
                for n in range(H):
                    if exists(b):
                        eng.wait_ge(a.t_ps, b * 16 + n + 1)
                        if n % HPS == 0 and (n >= 8 or after(b, 0)):
                            eng.wait_ge(a.pv, b * 4 + n // HPS - 1)
                        eng.activation(probs[:, n // HPS % 2, n % HPS, :, :].rearrange("p k q -> p (k q)"),
                                       ps[:, BANK_T[n % 3], :], ACT.Exp).then_inc(a.p_sb, 1)
                    if n == 1 and exists(b + 2):
                        eng.wait_ge(a.cT_ps, b + 3)
                        eng.activation(ctxT[:, :], ps[:, BANK_M, 0:S], ACT.Copy).then_inc(a.cT_sb, 1)
                    if n == 2 and exists(b):
                        max_copy(b, 1)
                    if n == 2 and exists(b - 1):
                        out_copy(b - 1, 1)
                    if n == 5 and exists(b + 2):
                        eng.wait_ge(a.qk_ps, b + 3)
                        if after(b, -2):
                            eng.wait_ge(a.to_dram, (b + 2) * 6 * DMA)
                        elif l == 0:
                            eng.wait_ge(bias_loaded, 8 * DMA)
                        eng.wait_ge(wT_sb, 6)
                        eng.activation(qk_hi[:, 0, :], ps[:, BANK_M, 0:S], ACT.Identity, bias=bq[l][:, 0:1])
                        eng.activation(qk_hi[:, 1, :], ps[:, BANK_M, S:2 * S], ACT.Identity,
                                       bias=bk[l][:, 0:1]).then_inc(a.qk_hi, 1)
                    if l == 1 and n == 7 and exists(b + 1):
                        eng.wait_ge(a.kT_ps, b + 2)
                        eng.activation(mask_k[1 - r][:, :, :].rearrange("p k q -> p (k q)"), ps[:, BANK_M, :],
                                       ACT.Copy).then_inc(a.kT_sb, 1)
                    if n == 8 and exists(b - 1):
                        eng.wait_ge(a.nT_ps, b)
                        eng.activation(o_normT[:, :], ps[:, BANK_O[1], 0:S], ACT.Copy).then_inc(a.nT_sb, 1)
                    if n == 10 and exists(b + 1):
                        max_copy(b + 1, 0)
                    if n == 10 and exists(b):
                        out_copy(b, 0)
                    if n == 12 and exists(b - 1):
                        s = (ln_a0, ln_a1)[l]
                        eng.wait_ge(s.xT, b)
                        if l == 0:
                            eng.activation(one(xnT_all, b - 1), ps[:, BANK_M, 0:S], ACT.Copy).then_inc(s.xs, 1)
                        else:
                            eng.wait_ge(a.r_ps, b - 1)
                            eng.wait_ge(a.x_hi, (b - 1) * 2)
                            eng.activation(r_x[:, :], ps[:, BANK_M, 0:S], ACT.Copy).then_inc(a.r_x, 1)
                    if l == 1 and n == 14 and exists(b - 1):
                        eng.wait_ge(a.r, (b - 1) * 10 + 1)
                        for i in range(NT):
                            last = eng.activation(r_e[:, i, :], ps[:, BANK_M, i * E:(i + 1) * E], ACT.Exp,
                                                  bias=r_nmax[:, i:i + 1], accum_out=r_sum[:, i:i + 1])
                        last.then_inc(a.r_exp, 1)

            def max_copy(b, half):
                eng.wait_ge(a.mT_ps, b * 2 + half + 1)
                if after(b, 0):
                    eng.wait_ge(a.m_in[half], b * 4 * DMA)
                elif l == 1:
                    eng.wait_ge(att[0].m_in[half], NB * 4 * DMA)
                eng.activation(maxT[:, half, :], ps[0:SETS * HPS, BANK_M, 0:S], ACT.Copy).then_inc(a.mT_sb, 1)

            def out_copy(b, half):
                eng.wait_ge(a.pv, b * 4 + 2 * half + 2)
                if after(b, 0):
                    eng.wait_ge(a.oT_ps, b * 2)
                eng.activation(o_raw[:, 2 * half:2 * half + 2, :].rearrange("p s q -> p (s q)"),
                               ps[:, BANK_O[half], :], ACT.Copy).then_inc(a.o_sb, 1)

            bodies(eng, body)

        def ffn_scalar(eng):
            def taps(b):
                for c in range(FC):
                    eng.wait_ge(h_ps, b * FC + c + 1)
                    if c == 0:
                        eng.wait_ge(h_act, b)
                    eng.activation(f_conv[:, c, :], ps[:, c, 0:S], ACT.Identity, scale=conv_w[:, c, 1:2],
                                   bias=conv_b[:, c:c + 1]).then_inc(h_tap, 1)

            def silu(b):
                eng.wait_ge(h_conv, b * 2 * FC + 2 * FC)
                eng.wait_ge(g_ps, b * NT)
                eng.activation(f_act[:, :, :].rearrange("p c t -> p (c t)"),
                               f_conv[:, :, :].rearrange("p c t -> p (c t)"), ACT.Silu).then_inc(h_act, 1)

            def rounding(b):
                for i in range(NT):
                    eng.wait_ge(g_stat, b * 8 + i * 4 + 4)
                    eng.activation(f_round[:, i, :], ps[:, 4 + i, :], ACT.Copy, scale=fa[:, i, 2:3],
                                   bias=ROUND).then_inc(g_round, 1)

            def int_copy(b):
                for i in range(NT):
                    eng.wait_ge(gi_ps, b * NT + i + 1)
                    eng.wait_ge(fy_ps, b)
                    eng.activation(f_intT[:, i, :, :].rearrange("p c t -> p (c t)"),
                                   ps[:, 6, i * 256:(i + 1) * 256].bitcast(BF16), ACT.Copy).then_inc(gi_sb, 1)

            def xT_copy(b):
                eng.wait_ge(ln_f0.xT, b + 1)
                eng.activation(one(xnT_all, b), ps[:, 7, S:2 * S], ACT.Copy).then_inc(ln_f0.xs, 1)

            taps(0)
            silu(0)

            def step(b):
                rounding(b)
                taps(b + 1)
                int_copy(b)
                silu(b + 1)
                xT_copy(b)

            batches(eng, step, NB - 1)
            rounding(NB - 1)
            int_copy(NB - 1)
            xT_copy(NB - 1)

        @block.scalar
        def _(eng):
            eng.wait_ge(wT_ps, 1)
            eng.activation(wq[0][:, :], ps[:, BANK_M, 0:D], ACT.Copy, scale=QSCALE).then_inc(wT_sb, 1)
            for n, w in enumerate((wk, wv, wo)):
                last = eng.activation(w[0][:, :], ps[:, BANK_M, (n + 1) * D:(n + 2) * D], ACT.Copy)
            last.then_inc(wT_sb, 1)
            eng.wait_ge(w_loaded, 8 * DMA)
            eng.activation(wq[1][:, :], w_raw[:, 4, :], ACT.Copy, scale=QSCALE).then_inc(wT_sb, 1)
            eng.wait_ge(bias_loaded, 8 * DMA)
            for l in range(2):
                eng.activation(bq[l][:, :], bq[l][:, :], ACT.Copy, scale=QSCALE).then_inc(wT_sb, 1)
            eng.wait_ge(wT_ps, 2)
            eng.activation(routerT[:, :], ps[:, BANK_M, 0:E], ACT.Copy).then_inc(wT_sb, 1)

            def pre_copy(b):
                eng.wait_ge(ln_pre.xT, b + 1)
                eng.activation(one(xnT_all, b), ps[:, BANK_M, 0:S], ACT.Copy).then_inc(ln_pre.xs, 1)

            batches(eng, pre_copy)
            attention_scalar(eng, 0)
            if stages >= 2:
                for c in range(FC // 2):
                    eng.wait_ge(f_wT_ps, c + 1)
                eng.activation(w1T[:, :, :].rearrange("p c h -> p (c h)"), ps[:, 0, :], ACT.Copy).then_inc(f_wT_sb, 1)
                eng.activation(w2T[:, :, :].rearrange("p c h -> p (c h)"), ps[:, 1, :], ACT.Copy).then_inc(f_wT_sb, 1)
                eng.wait_ge(f_tern, 9)
                ffn_scalar(eng)
            if stages >= 3:
                attention_scalar(eng, 1)
            if stages >= 4:
                for e in range(E):
                    eng.wait_ge(fc_ps, 2 * e + 1)
                    eng.activation(fc1_hi[:, e, :, :].rearrange("p c h -> p (c h)"), ps[:, 2 * (e % 2), :],
                                   ACT.Copy).then_inc(fc_hi, 1)
                    eng.wait_ge(fc_ps, 2 * e + 2)
                    eng.activation(fc2T[:, e, :, :].rearrange("p c d -> p (c d)"), ps[:, 2 * (e % 2) + 1, :],
                                   ACT.Copy).then_inc(fc_hi, 1)
                with eng.Fori(0, NG) as g:
                    for e in range(E):
                        for c in range(EC):
                            u = g * E + e
                            eng.wait_ge(fc1_ps, u * EC + c + 1)
                            if c == 0:
                                eng.wait_ge(y_ps, u + 1)
                            eng.activation(hT[:, e % 2, c, :], ps[:, c, :], ACT.Silu).then_inc(h_sb, 1)

        def attention_vector(eng, l):
            a = att[l]
            s = (ln_a0, ln_a1)[l]

            def body(b, r):
                for n in range(H):
                    if exists(b + 1):
                        eng.wait_ge(a.s_ps, (b + 1) * 16 + n + 1)
                        eng.tensor_reduce(neg_max[:, :, n], ps[:, BANK_S[n % 2], :].rearrange("p (i k) -> p i k", i=NT),
                                          AX.X, ALU.max, negate=True).then_inc(a.s_max, 1)
                    if n == 0 and exists(b + 1):
                        eng.wait_ge(a.v_ps, b + 2)
                        if exists(b - 1):
                            eng.wait_ge(a.pv, b * 4)
                        elif l == 1:
                            eng.wait_ge(att[0].pv, NB * 4)
                        eng.tensor_tensor(v_aug[1 - r][:, :, :, 0:DH],
                                          ps[:, BANK_M, 0:NT * D].rearrange("p (i h d) -> p i h d", i=NT, d=DH),
                                          bv[l][:, :].rearrange("p (h d) -> p h d", d=DH)[:, None, :, :]
                                          .to_broadcast([P, NT, H, DH]), ALU.add).then_inc(a.v_sb, 1)
                    if l == 1 and n == 3 and exists(b + 2):
                        eng.wait_ge(a.k_in, (b + 3) * DMA)
                        if exists(b):
                            eng.wait_ge(a.s_ps, (b + 1) * 16)
                            eng.wait_ge(a.kT_ps, b + 1)
                        eng.tensor_scalar(mask_q[r][:, :, :], mask_in[:, :, :], MASK_B, None,
                                          ALU.mult).then_inc(a.k_q, 1)
                    if n in (4, 6) and exists(b - 1):
                        i = (n - 4) // 2
                        t = b - 1
                        o_view = ps[:, BANK_O[1], :].rearrange("p (h r) -> p h r", r=HR)
                        eng.wait_ge(a.oT_ps, t * 2 + i + 1)
                        eng.reciprocal(rden[:, i, :], o_view[:, :, DH]).then_inc(a.rden, 1)
                        eng.wait_ge(a.rden, t * 2 + i + 1)
                        if i == 0:
                            eng.wait_ge(a.nT_ps, t)
                        eng.tensor_tensor(o_norm[:, i, :].rearrange("p (h d) -> p h d", d=DH), o_view[:, :, 0:DH],
                                          rden[:, i, :, None].to_broadcast([P, H, DH]), ALU.mult).then_inc(a.o_norm, 1)
                    if n == 5 and exists(b + 2):
                        eng.wait_ge(a.qk_hi, b + 3)
                        for w, bias in ((0, bq[l]), (1, bk[l])):
                            last = eng.scalar_tensor_tensor(out=qk_lo[:, w, :], in0=ps[:, BANK_M, w * S:(w + 1) * S],
                                                            scalar=bias[:, 0:1], in1=qk_hi[:, w, :].bitcast(F32),
                                                            op0=ALU.add, op1=ALU.subtract)
                        last.then_inc(a.qk_lo, 1)
                    if n == 8 and exists(b + 1):
                        max_parts(b + 1, 0)
                    if n == 9 and exists(b - 1):
                        eng.wait_ge(a.y_ps, b)
                        eng.wait_ge((ln_pre, ln_f0)[l].q, b)
                        eng.tensor_tensor(x_tiles(b - 1), ps[:, BANK_O[1], S:2 * S].rearrange("p (i d) -> p i d", i=NT),
                                          x_tiles(b - 1), ALU.add).then_inc(a.x_new, 1)
                        ln_stats(eng, s, b - 1, (a.x_new, b))
                    if n == 11 and exists(b - 1):
                        ln_apply(eng, s, b - 1)
                        if l == 0:
                            quantise_rows(eng, s, b - 1)
                    if l == 1 and n == 12 and exists(b - 1):
                        eng.wait_ge(a.r_x, b)
                        eng.tensor_copy(one(xhT_all, b - 1), r_x[:, :]).then_inc(a.x_hi, 1)
                        eng.wait_ge(a.x_hi, (b - 1) * 2 + 1)
                        eng.tensor_tensor(one(xlT_all, b - 1), r_x[:, :], one(xhT_all, b - 1).bitcast(F32),
                                          ALU.subtract).then_inc(a.x_hi, 1)
                    if l == 1 and n == 13 and exists(b - 1):
                        eng.wait_ge(a.r_ps, b)
                        eng.tensor_reduce(r_nmax[:, :], ps[:, BANK_M, 0:NT * E].rearrange("p (i e) -> p i e", i=NT),
                                          AX.X, ALU.max, negate=True).then_inc(a.r, 1)
                    if l == 1 and n == 15 and exists(b - 1):
                        routing(b - 1)
                if exists(b + 1):
                    max_parts(b + 1, 1)

            def max_parts(b, half):
                eng.wait_ge(a.s_max, b * 16 + half * 8 + 8)
                if after(b, 0):
                    eng.wait_ge(a.mT_ps, b * 2)
                for i in range(NT):
                    src = neg_max[:, i, half * 8:half * 8 + 8].rearrange("p (s j) -> p s j", j=HPS)
                    last = eng.tensor_copy(max_split[:, i, half, :, 0, :], src)
                last.then_inc(a.m_hi, 1)
                eng.wait_ge(a.m_hi, b * 2 + half + 1)
                for i in range(NT):
                    src = neg_max[:, i, half * 8:half * 8 + 8].rearrange("p (s j) -> p s j", j=HPS)
                    last = eng.tensor_tensor(max_split[:, i, half, :, 1, :], src,
                                             max_split[:, i, half, :, 0, :].bitcast(F32), ALU.subtract)
                last.then_inc(a.m_split, 1)

            def routing(b):
                n = b * 10
                eng.wait_ge(a.r_exp, b + 1)
                eng.reciprocal(r_sum[:, :], r_sum[:, :]).then_inc(a.r, 1)
                eng.wait_ge(a.r, n + 2)
                eng.tensor_tensor(r_e[:, :, :], r_e[:, :, :], r_sum[:, :, None].to_broadcast([P, NT, E]),
                                  ALU.mult).then_inc(a.r, 1)
                hold(eng, a.r, n + 3)
                for i in range(NT):
                    last = eng.max(r_top[:, i, :], r_e[:, i, :])
                last.then_inc(a.r, 1)
                hold(eng, a.r, n + 4)
                for i in range(NT):
                    eng.max_index(r_idx[:, i, :], r_top[:, i, :], r_e[:, i, :])
                eng.tensor_tensor(r_den[:, :], r_top[:, :, 0], r_top[:, :, 1], ALU.add).then_inc(a.r, 1)
                eng.wait_ge(a.r, n + 5)
                eng.tensor_scalar(r_den[:, :], r_den[:, :], 1e-9, None, ALU.max).then_inc(a.r, 1)
                eng.tensor_copy(r_idf[:, :, :], r_idx[:, :, 0:2])
                eng.wait_ge(a.r, n + 6)
                eng.reciprocal(r_den[:, :], r_den[:, :]).then_inc(a.r, 1)
                eng.wait_ge(a.r, n + 7)
                eng.tensor_tensor(r_w[:, :, :], r_top[:, :, 0:2], r_den[:, :, None].to_broadcast([P, NT, 2]),
                                  ALU.mult).then_inc(a.r, 1)
                eng.wait_ge(a.r, n + 8)
                for k in range(2):
                    for i in range(NT):
                        last = eng.tensor_scalar(r_pick[:, k, i, :], iota_e[:, :], r_idf[:, i, k:k + 1], r_w[:, i, k:k + 1],
                                                 ALU.is_equal, ALU.mult)
                last.then_inc(a.r, 1)
                eng.wait_ge(a.r, n + 9)
                eng.tensor_tensor(w_te[:, bass.ds(b * NT, NT), :], r_pick[:, 0, :, :], r_pick[:, 1, :, :],
                                  ALU.add).then_inc(a.r, 1)

            bodies(eng, body)

        def ffn_vector(eng):
            def conv(b):
                for c in range(FC):
                    eng.wait_ge(h_tap, b * FC + c + 1)
                    eng.scalar_tensor_tensor(out=f_conv[:, c, 1:S], in0=ps[:, c, 0:S - 1], scalar=conv_w[:, c, 0:1],
                                             in1=f_conv[:, c, 1:S], op0=ALU.mult, op1=ALU.add).then_inc(h_conv, 1)
                for c in range(FC):
                    eng.wait_ge(h_conv, b * 2 * FC + c + 1)
                    eng.scalar_tensor_tensor(out=f_conv[:, c, 0:S - 1], in0=ps[:, c, 1:S], scalar=conv_w[:, c, 2:3],
                                             in1=f_conv[:, c, 0:S - 1], op0=ALU.mult, op1=ALU.add).then_inc(h_conv, 1)

            def quant_scale(b):
                for i in range(NT):
                    n = b * 8 + i * 4
                    eng.wait_ge(g_ps, b * NT + i + 1)
                    if i == 0:
                        eng.wait_ge(fx_new, b)
                    eng.tensor_reduce(fa[:, i, 0:1], ps[:, 4 + i, :], AX.X, ALU.max,
                                      apply_absolute_value=True).then_inc(g_stat, 1)
                    eng.wait_ge(g_stat, n + 1)
                    eng.tensor_scalar(fa[:, i, 0:1], fa[:, i, 0:1], QUANT_EPS, None, ALU.max).then_inc(g_stat, 1)
                    eng.wait_ge(g_stat, n + 2)
                    eng.reciprocal(fa[:, i, 1:2], fa[:, i, 0:1])
                    eng.tensor_scalar(fa[:, i, 3:4], fa[:, i, 0:1], wq_stat[:, 5:6], None, ALU.mult).then_inc(g_stat, 1)
                    eng.wait_ge(g_stat, n + 3)
                    eng.tensor_scalar(fa[:, i, 2:3], fa[:, i, 1:2], 127.0, None, ALU.mult).then_inc(g_stat, 1)

            def quant_clip(b):
                for i in range(NT):
                    eng.wait_ge(g_round, b * NT + i + 1)
                    eng.wait_ge(gi_ps, b * NT)
                    eng.tensor_scalar(f_round[:, i, :], f_round[:, i, :], ROUND, 127.0, ALU.subtract,
                                      ALU.min).then_inc(g_int, 1)
                    eng.wait_ge(g_int, b * 2 * NT + i * 2 + 1)
                    eng.tensor_scalar(f_int[:, i, :], f_round[:, i, :], -128.0, None, ALU.max).then_inc(g_int, 1)

            def residual(b):
                eng.wait_ge(fy_ps, b + 1)
                for i in range(NT):
                    last = eng.scalar_tensor_tensor(out=x_tile(b, i), in0=ps[:, 7, i * P:(i + 1) * P],
                                                    scalar=fa[:, i, 3:4], in1=x_tile(b, i), op0=ALU.mult, op1=ALU.add)
                last.then_inc(fx_new, 1)
                ln_stats(eng, ln_f0, b, (fx_new, b + 1))

            conv(0)

            def step(b):
                quant_scale(b)
                quant_clip(b)
                conv(b + 1)
                residual(b)
                ln_apply(eng, ln_f0, b, bo[1])

            batches(eng, step, NB - 1)
            quant_scale(NB - 1)
            quant_clip(NB - 1)
            residual(NB - 1)
            ln_apply(eng, ln_f0, NB - 1, bo[1])

        @block.vector
        def _(eng):
            for r in range(2):
                eng.memset(k_blocks[r][:, :, :, :].bitcast(F32), 0.0).then_inc(cast_ready, 1)
            eng.wait_ge(const_ready, 3)
            eng.tensor_copy(ident_bf[:, :], ident[:, :]).then_inc(cast_ready, 1)
            eng.tensor_scalar(neg_mask_eye[:, :], ident[:, :], -MASK_A, None, ALU.mult).then_inc(cast_ready, 1)
            eng.wait_ge(cast_ready, 2)
            for r in range(2):
                for j in range(HPS):
                    last = eng.memset(k_blocks[r][j * HR:j * HR + 2, :, j, :].bitcast(F32), 1.0)
                last.then_inc(stack_zeroed, 1)
            eng.wait_ge(bias_loaded, 8 * DMA)

            def pre_norm(b):
                ln_stats(eng, ln_pre, b, (x_loaded, DMA))
                ln_apply(eng, ln_pre, b, bo[0])

            batches(eng, pre_norm)
            eng.wait_ge(ffn_loaded, 5 * DMA)
            for w in range(2):
                eng.tensor_reduce(wq_stat[:, w:w + 1], ffn_raw[:, w, :, :], AX.XY, ALU.add,
                                  apply_absolute_value=True).then_inc(f_stat, 1)
            eng.wait_ge(f_mean, 1)
            eng.tensor_scalar(wq_stat[:, 2:4], ps[:, BANK_M, 0:2], QUANT_EPS, None, ALU.max).then_inc(f_tern, 1)
            eng.wait_ge(f_tern, 1)
            eng.reciprocal(wq_stat[:, 6:8], wq_stat[:, 2:4]).then_inc(f_tern, 1)
            eng.tensor_scalar(wq_stat[:, 5:6], wq_stat[:, 3:4], 1.0 / 127.0, None, ALU.mult).then_inc(f_tern, 1)
            eng.wait_ge(f_tern, 3)
            for w in range(2):
                eng.tensor_scalar(ffn_raw[:, w, :, :], ffn_raw[:, w, :, :], wq_stat[:, 6 + w:7 + w], ROUND,
                                  ALU.mult, ALU.add).then_inc(f_tern, 1)
            eng.wait_ge(f_tern, 5)
            for w in range(2):
                eng.tensor_scalar(ffn_raw[:, w, :, :], ffn_raw[:, w, :, :], ROUND, 1.0, ALU.subtract,
                                  ALU.min).then_inc(f_tern, 1)
            eng.wait_ge(f_tern, 7)
            eng.tensor_scalar(ffn_raw[:, :, :, :], ffn_raw[:, :, :, :], -1.0, None, ALU.max).then_inc(f_tern, 1)
            eng.tensor_scalar(conv_w[:, :, :], conv_w[:, :, :], wq_stat[:, 2:3], None, ALU.mult).then_inc(f_tern, 1)
            attention_vector(eng, 0)
            if stages >= 2:
                ffn_vector(eng)
            if stages >= 3:
                attention_vector(eng, 1)
            if stages >= 4:
                for e in range(E):
                    eng.wait_ge(fc_hi, 2 * e + 1)
                    eng.tensor_tensor(fc1_lo[:, e, :, :].rearrange("p c h -> p (c h)"), ps[:, 2 * (e % 2), :],
                                      fc1_hi[:, e, :, :].rearrange("p c h -> p (c h)").bitcast(F32),
                                      ALU.subtract).then_inc(fc_done, 1)
                eng.sem_inc(y_used, 2)
                with eng.Fori(0, NG) as g:
                    for e in range(E):
                        u = g * E + e
                        eng.wait_ge(y_ps, u + 3)
                        eng.wait_ge(y_used, u + 2)
                        for i in range(GT):
                            tile = g * GT + i
                            xt = x_res[:, bass.ds(tile, 1), :].rearrange("p o d -> p (o d)")
                            wt = w_te[:, bass.ds(tile, 1), e:e + 1].rearrange("p o d -> p (o d)")
                            last = eng.scalar_tensor_tensor(out=xt, in0=ps[:, 4 + e % 2, i * P:(i + 1) * P], scalar=wt,
                                                            in1=xt, op0=ALU.mult, op1=ALU.add)
                        last.then_inc(y_used, 1)

        def attention_tensor(eng, l):
            a = att[l]
            s = (ln_a0, ln_a1)[l]
            src_ln = (ln_pre, ln_f0)[l]

            def body(b, r):
                if exists(b) :
                    eng.wait_ge(a.mT_sb, b * 2 + 1)
                if exists(b - 2):
                    if l == 0:
                        eng.wait_ge(s.xs, b - 1)
                    else:
                        eng.wait_ge(a.r_exp, b - 1)
                for n in range(H):
                    if exists(b + 1):
                        scores(b + 1, 1 - r, n)
                    if n % HPS == 1:
                        if n == 1:
                            if exists(b - 1):
                                weighted_v(b - 1, 1 - r, 3)
                        elif exists(b):
                            weighted_v(b, r, n // HPS - 1)
                    if exists(b):
                        shifted(b, r, n)
                    extras(b, r, n)

            def scores(b, r, n):
                st, j = n // HPS, n % HPS
                if n % 8 == 0:
                    eng.wait_ge(a.stack[n // 8], (b + 1) * 8 * DMA)
                if l == 1 and n == 0:
                    eng.wait_ge(a.k_q, b + 1)
                if n >= 2 or after(b, 0):
                    eng.wait_ge(a.s_max, b * 16 + n - 1)
                bank = BANK_S[n % 2]
                if l == 1:
                    eng.matmul(ps[:, bank, :], neg_mask_eye[:, :], mask_q[r][:, :, :].rearrange("p i k -> p (i k)"),
                               start=True, stop=False)
                for i in range(NT):
                    mm = eng.matmul(ps[:, bank, i * S:(i + 1) * S], q_stack[r][:, st, i * P:(i + 1) * P],
                                    k_blocks[r][:, st, j, :], start=(l == 0), stop=(l == 0 or i == NT - 1))
                mm.then_inc(a.s_ps, 1)

            def shifted(b, r, n):
                st, j = n // HPS, n % HPS
                if n % 8 == 0:
                    eng.wait_ge(a.m_in[n // 8], (b + 1) * 4 * DMA)
                if l == 1 and n == 0:
                    eng.wait_ge(a.kT_sb, b + 1)
                back = 3 if n >= 3 else (1, 3, 2)[n]
                if n >= 3 or after(b, 0):
                    eng.wait_ge(a.p_sb, b * 16 + n - back + 1)
                bank = BANK_T[n % 3]
                if l == 1:
                    eng.matmul(ps[:, bank, :], neg_mask_eye[:, :], mask_k[r][:, :, :].rearrange("p i k -> p (i k)"),
                               start=True, stop=False)
                for k in range(NT):
                    mm = eng.matmul(ps[:, bank, k * S:(k + 1) * S], k_blocks[r][:, st, j, k * P:(k + 1) * P],
                                    q_stack[r][:, st, :], start=(l == 0), stop=(l == 0 or k == NT - 1))
                mm.then_inc(a.t_ps, 1)

            def weighted_v(b, r, st):
                eng.wait_ge(a.p_sb, b * 16 + st * HPS + HPS)
                if st == 0:
                    eng.wait_ge(a.v_sb, b + 1)
                    if after(b, 0):
                        eng.wait_ge(a.o_sb, b * 2 - 1)
                if st == 2 and (after(b, 0)):
                    eng.wait_ge(a.x_new, b)
                bank = BANK_O[st // 2]
                col = st % 2 * S
                for k in range(NT):
                    for j in range(HPS):
                        mm = eng.matmul(ps[j * HR:(j + 1) * HR, bank, col:col + S], v_aug[r][:, k, st * HPS + j, :],
                                        probs[:, st % 2, j, k, :], start=(k == 0), stop=(k == NT - 1),
                                        tile_position=(0, j * HR))
                mm.then_inc(a.pv, 1)

            def extras(b, r, n):
                M = BANK_M
                if n == 0 and exists(b + 1):
                    eng.wait_ge(a.cT_sb, b + 2)
                    for i in range(NT):
                        mm = eng.matmul(ps[:, M, i * D:(i + 1) * D], ctxT[:, i * P:(i + 1) * P], wv[l][:, :],
                                        start=True, stop=True)
                    mm.then_inc(a.v_ps, 1)
                if n == 1 and exists(b + 2):
                    eng.wait_ge(a.ctx_in, (b + 3) * DMA)
                    if after(b, -2):
                        eng.wait_ge(a.v_sb, b + 2)
                    for i in range(NT):
                        mm = eng.transpose(ps[:, M, i * P:(i + 1) * P], ctx_in[:, i, :], ident[:, :])
                    mm.then_inc(a.cT_ps, 1)
                if n == 2 and exists(b):
                    if exists(b + 2):
                        eng.wait_ge(a.cT_sb, b + 3)
                    elif exists(b + 1):
                        eng.wait_ge(a.v_sb, b + 2)
                    max_transposes(b, 1)
                if n in (3, 5) and exists(b - 1):
                    i = (n - 3) // 2
                    if i == 0:
                        eng.wait_ge(a.o_sb, b * 2)
                    else:
                        eng.wait_ge(a.o_norm, b * 2 - 1)
                    for st in range(SETS):
                        mm = eng.transpose(ps[:, BANK_O[1], st * P:(st + 1) * P], o_raw[:, st, i * P:(i + 1) * P],
                                           ident[:, :])
                    mm.then_inc(a.oT_ps, 1)
                if n == 4 and exists(b + 2):
                    if exists(b):
                        eng.wait_ge(a.mT_sb, b * 2 + 2)
                    else:
                        eng.wait_ge(a.cT_sb, b + 3)
                    if l == 0 or not after(b, -2):
                        eng.wait_ge(src_ln.xs, b + 3 if l == 0 else NB)
                    xT = xnT_all[:, bass.ds(b + 2, 1), :].rearrange("p o t -> p (o t)")
                    eng.matmul(ps[:, M, 0:S], wq[l][:, :], xT, start=True, stop=True)
                    eng.matmul(ps[:, M, S:2 * S], wk[l][:, :], ctxT[:, :], start=True, stop=True).then_inc(a.qk_ps, 1)
                if l == 1 and n == 6 and exists(b + 1):
                    if exists(b + 2):
                        eng.wait_ge(a.qk_lo, b + 3)
                    elif exists(b):
                        eng.wait_ge(a.mT_sb, b * 2 + 2)
                    eng.wait_ge(a.k_q, b + 2)
                    for k in range(NT):
                        for i in range(NT):
                            mm = eng.transpose(ps[:, M, k * S + i * P:k * S + (i + 1) * P],
                                               mask_q[1 - r][:, i, k * P:(k + 1) * P].bitcast(F32), ident[:, :])
                    mm.then_inc(a.kT_ps, 1)
                if n == 7 and exists(b - 1):
                    eng.wait_ge(a.o_norm, b * 2)
                    for i in range(NT):
                        mm = eng.transpose(ps[:, BANK_O[1], i * P:(i + 1) * P], o_norm[:, i, :], ident[:, :])
                    mm.then_inc(a.nT_ps, 1)
                if n == 8 and exists(b - 1):
                    eng.wait_ge(a.nT_sb, b)
                    for i in range(NT):
                        mm = eng.matmul(ps[:, BANK_O[1], S + i * D:S + (i + 1) * D], o_normT[:, i * P:(i + 1) * P],
                                        wo[l][:, :], start=True, stop=True)
                    mm.then_inc(a.y_ps, 1)
                if n == 9 and exists(b + 1):
                    if l == 1:
                        eng.wait_ge(a.kT_sb, b + 2)
                    elif exists(b + 2):
                        eng.wait_ge(a.qk_lo, b + 3)
                    elif exists(b):
                        eng.wait_ge(a.mT_sb, b * 2 + 2)
                    max_transposes(b + 1, 0)
                if n == 11 and exists(b - 1):
                    if exists(b + 1):
                        eng.wait_ge(a.mT_sb, b * 2 + 3)
                    elif exists(b):
                        eng.wait_ge(a.mT_sb, b * 2 + 2)
                    ready = (s.q, b * 6) if l == 0 else (s.xn, b)
                    xn_transposes(eng, s, b - 1, M, 0, ready)
                if l == 1 and n == 13 and exists(b - 1):
                    eng.wait_ge(a.r_x, b)
                    for i in range(NT):
                        mm = eng.matmul(ps[:, M, i * E:(i + 1) * E], r_x[:, i * P:(i + 1) * P], routerT[:, :],
                                        start=True, stop=True)
                    mm.then_inc(a.r_ps, 1)

            def max_transposes(b, half):
                eng.wait_ge(a.m_split, b * 2 + half + 1)
                for i in range(NT):
                    mm = eng.transpose(ps[0:SETS * HPS, BANK_M, i * P:(i + 1) * P],
                                       max_split[:, i, half, :, :, :].bitcast(F32).rearrange("p s m j -> p (s m j)"),
                                       ident[:, :])
                mm.then_inc(a.mT_ps, 1)

            bodies(eng, body)

        def ffn_tensor(eng):
            def hidden(b):
                for c in range(FC):
                    eng.wait_ge(h_conv, b * 2 * FC)
                    eng.matmul(ps[:, c, 0:S], w1T[:, c, :], one(xnT_all, b), start=True, stop=True).then_inc(h_ps, 1)

            def act_transposes(b):
                eng.wait_ge(h_act, b + 1)
                for i in range(NT):
                    eng.wait_ge(g_round, b * NT)
                    for c in range(FC):
                        mm = eng.transpose(ps[:, 4 + i, c * P:(c + 1) * P], f_act[:, c, i * P:(i + 1) * P], ident[:, :])
                    mm.then_inc(g_ps, 1)

            def int_transposes(b):
                for i in range(NT):
                    eng.wait_ge(g_int, b * 2 * NT + 2 * i + 2)
                    eng.wait_ge(gi_sb, b * NT + i)
                    bank = ps[:, 6, i * 256:(i + 1) * 256].bitcast(BF16)
                    for c in range(FC):
                        mm = eng.transpose(bank[:, c * P:(c + 1) * P], f_int[:, i, c * P:(c + 1) * P], ident_bf[:, :])
                    mm.then_inc(gi_ps, 1)

            def output(b):
                eng.wait_ge(gi_sb, b * NT + NT)
                eng.wait_ge(ln_f0.xs, b)
                for i in range(NT):
                    for c in range(FC):
                        mm = eng.matmul(ps[:, 7, i * P:(i + 1) * P], f_intT[:, i, c, :], w2T[:, c, :],
                                        start=(c == 0), stop=(c == FC - 1))
                mm.then_inc(fy_ps, 1)

            hidden(0)

            def step(b):
                act_transposes(b)
                hidden(b + 1)
                int_transposes(b)
                output(b)
                xn_transposes(eng, ln_f0, b, 7, S, (ln_f0.xn, b + 1))

            batches(eng, step, NB - 1)
            act_transposes(NB - 1)
            int_transposes(NB - 1)
            output(NB - 1)
            xn_transposes(eng, ln_f0, NB - 1, 7, S, (ln_f0.xn, NB))

        @block.tensor
        def _(eng):
            eng.wait_ge(const_ready, 3)
            eng.wait_ge(w_loaded, 8 * DMA)
            for n in range(4):
                mm = eng.transpose(ps[:, BANK_M, n * D:(n + 1) * D], w_raw[:, n, :], ident[:, :])
            mm.then_inc(wT_ps, 1)
            eng.wait_ge(ffn_loaded, 5 * DMA)
            eng.wait_ge(wT_sb, 2)
            eng.transpose(ps[:, BANK_M, 0:E], router_raw[:, :], ident[0:E, 0:E]).then_inc(wT_ps, 1)
            eng.wait_ge(wT_sb, 6)

            def pre_transposes(b):
                eng.wait_ge(ln_pre.xs, b)
                xn_transposes(eng, ln_pre, b, BANK_M, 0, (ln_pre.xn, b + 1))

            batches(eng, pre_transposes)
            eng.wait_ge(const_ready, 5)
            eng.wait_ge(ln_pre.xs, NB)
            eng.wait_ge(f_stat, 2)
            eng.matmul(ps[:, BANK_M, 0:2], mean_ones[:, :], wq_stat[:, 0:2], start=True, stop=True).then_inc(f_mean, 1)
            eng.wait_ge(f_tern, 1)
            attention_tensor(eng, 0)
            if stages >= 2:
                eng.wait_ge(f_tern, 8)
                eng.wait_ge(att[0].s_max, NB * 16)
                for w in range(2):
                    for c in range(FC):
                        mm = eng.transpose(ps[:, w, c * P:(c + 1) * P], ffn_raw[:, w, c, :], ident[:, :])
                    mm.then_inc(f_wT_ps, 1)
                eng.wait_ge(f_wT_sb, 2)
                eng.wait_ge(att[0].p_sb, NB * 16)
                eng.wait_ge(att[0].x_new, NB)
                eng.wait_ge(ln_a0.xs, NB)
                ffn_tensor(eng)
            if stages >= 3:
                eng.wait_ge(ln_f0.xs, NB)
                attention_tensor(eng, 1)
            if stages >= 4:
                eng.wait_ge(att[1].x_new, NB)
                for e in range(E):
                    eng.wait_ge(fc_loaded[e % 2], (e // 2 + 1) * 2 * DMA)
                    if e >= 2:
                        eng.wait_ge(fc_done, e - 1)
                        eng.wait_ge(fc_hi, (e - 1) * 2)
                    for c in range(EC):
                        mm = eng.transpose(ps[:, 2 * (e % 2), c * P:(c + 1) * P], fc_raw[:, e % 2, 0, c * P:(c + 1) * P],
                                           ident[:, :])
                    mm.then_inc(fc_ps, 1)
                    for c in range(EC):
                        mm = eng.transpose(ps[:, 2 * (e % 2) + 1, c * P:(c + 1) * P],
                                           fc_raw[:, e % 2, 1, c * P:(c + 1) * P], ident[:, :])
                    mm.then_inc(fc_ps, 1)
                eng.wait_ge(fc_hi, 2 * E)
                eng.wait_ge(fc_done, E)
                eng.wait_ge(att[1].x_hi, NB * 2)
                eng.wait_ge(att[1].r, NB * 10)
                eng.sem_inc(y_ps, 2)

                def up(g, e, c):
                    if e > 0 or after(g, 0):
                        eng.wait_ge(h_sb, (g * E + e - 1) * EC + c + 1)
                    xh = xhT_all[:, :, :].rearrange("p b t -> p (b t)")[:, bass.ds(g * GT * P, GT * P)]
                    xl = xlT_all[:, :, :].rearrange("p b t -> p (b t)")[:, bass.ds(g * GT * P, GT * P)]
                    eng.matmul(ps[:, c, :], fc1_hi[:, e, c, :], xh, start=True, stop=False)
                    eng.matmul(ps[:, c, :], fc1_hi[:, e, c, :], xl, start=False, stop=False)
                    eng.matmul(ps[:, c, :], fc1_lo[:, e, c, :], xh, start=False, stop=True).then_inc(fc1_ps, 1)

                def down(g, e, i):
                    u = g * E + e
                    if i == 0:
                        eng.wait_ge(h_sb, u * EC + EC)
                        eng.wait_ge(y_used, u + 1)
                    for c in range(EC):
                        mm = eng.matmul(ps[:, 4 + e % 2, i * P:(i + 1) * P], hT[:, e % 2, c, i * P:(i + 1) * P],
                                        fc2T[:, e, c, :], start=(c == 0), stop=(c == EC - 1))
                    if i == GT - 1:
                        mm.then_inc(y_ps, 1)

                def group(g):
                    for e in range(E):
                        for c in range(EC):
                            up(g, e, c)
                            if e > 0:
                                down(g, e - 1, c)
                    for i in range(GT):
                        down(g, E - 1, i)

                group(0)
                with eng.Fori(1, NG) as g:
                    group(g)


_INPUTS = (
    ["x", "ctx_1024", "mask_Bx1xSxS2_ik1"]
    + [f"L0_xattn_{n}" for n in ("Wq", "bq", "Wk", "bk", "Wv", "bv", "Wo", "bo")]
    + ["L0_ffn_w1", "L0_ffn_conv_w", "L0_ffn_conv_b", "L0_ffn_w2"]
    + [f"L1_xattn_{n}" for n in ("Wq", "bq", "Wk", "bk", "Wv", "bv", "Wo", "bo")]
    + ["L1_ffn_router_w", "L1_ffn_fc1_w", "L1_ffn_fc2_w"]
)


def kernel(**inputs):
    import concourse.bacc as bacc
    from concourse.bass_utils import run_bass_kernel_spmd

    nc = bacc.Bacc("TRN2", target_bir_lowering=False, num_devices=1)
    arrays, aps = {}, {}
    for name in _INPUTS:
        a = np.ascontiguousarray(inputs[name])
        arrays[name] = a
        aps[name] = nc.dram_tensor(name, a.shape, mybir.dt.from_np(a.dtype), kind="ExternalInput").ap()
    out = nc.dram_tensor("out", inputs["x"].shape, F32, kind="ExternalOutput").ap()
    build(nc, aps, out)
    r = run_bass_kernel_spmd(nc, [arrays], core_ids=[0])
    return r.results[0]["out"]
```

```python
import numpy as np
import concourse.bass as bass
from concourse import mybir
from contextlib import ExitStack

F32 = mybir.dt.float32
F32R = mybir.dt.float32r
BF16 = mybir.dt.bfloat16
I32 = mybir.dt.int32
U32 = mybir.dt.uint32
ALU = mybir.AluOpType
ACT = mybir.ActivationFunctionType
AX = mybir.AxisListType

P = 128
DMA = 16
LN_EPS = 1e-5
QUANT_EPS = 1e-5
ROUND = 1.5 * 2.0 ** 23
MASK_A, MASK_B = 625.0 * 512.0, 3125.0
assert MASK_A * MASK_B == 1e9


AT = [{"a_ctx": 2,
  "a_k_hi": 6,
  "a_mask": 99,
  "a_max0": 10,
  "a_max1": 0,
  "a_norm": 7,
  "a_out0": 10,
  "a_out1": 0,
  "a_q_hi": 4,
  "a_qk": 4,
  "a_v": 9,
  "ctx": 2,
  "d_ln": 11,
  "d_norm": 4,
  "d_quant": [12, 13, 14],
  "d_res": 9,
  "mask": 99,
  "max0": 10,
  "max1": 0,
  "normT": 7,
  "outT": 3,
  "pv": 5,
  "qk": 4,
  "v": 6,
  "x": 15,
  "y": 8},
 {"a_ctx": 2,
  "a_k_hi": 6,
  "a_mask": 9,
  "a_max0": 12,
  "a_max1": 2,
  "a_norm": 7,
  "a_out0": 10,
  "a_out1": 2,
  "a_q_hi": 5,
  "a_qk": 3,
  "a_v": 6,
  "ctx": 3,
  "d_ln": 12,
  "d_norm": 3,
  "d_quant": [],
  "d_res": 9,
  "mask": 8,
  "max0": 11,
  "max1": 0,
  "normT": 7,
  "outT": 3,
  "pv": 5,
  "qk": 3,
  "v": 5,
  "x": 14,
  "y": 8}]


def build(nc, inp, out, stages=4):
    NB, S, D = inp["x"].shape
    NT = S // P
    H = 16
    DH = D // H
    SETS, HPS = 4, 4
    HR = P // HPS
    FF = inp["L0_ffn_w1"].shape[0]
    FC = FF // P
    E, EH, _ = inp["L1_ffn_fc1_w"].shape
    EC = EH // P
    GT = 4
    NG = NB * NT // GT
    QSCALE = float(1.0 / np.sqrt(np.float32(DH)))
    assert D == P and DH * H == D and SETS * HPS == H

    with ExitStack() as ctx:
        def sb(name, shape, dt=F32):
            return ctx.enter_context(nc.sbuf_tensor(name, shape, dt))

        def sem(name):
            return ctx.enter_context(nc.semaphore(name))

        ps = ctx.enter_context(nc.psum_tensor("ps", [P, 8, 512], F32))
        BANK_S = (0, 1)
        BANK_T = (2, 3, 4)
        BANK_O = (5, 6)
        BANK_M = 7

        ident = sb("ident", [P, P])
        ident_bf = sb("ident_bf", [P, P], BF16)
        neg_mask_eye = sb("neg_mask_eye", [P, P], F32R)
        mean_ones = sb("mean_ones", [P, P])
        minus_half = sb("minus_half", [P, NB * NT])
        zeros = sb("zeros", [P, S])
        iota_e = sb("iota_e", [P, E])

        x_res = sb("x_res", [P, NB * NT, D])
        xnT_all = sb("xnT_all", [P, NB, S])
        xhT_all = sb("xhT_all", [P, NB, S], F32R)
        xlT_all = sb("xlT_all", [P, NB, S], F32R)
        w_te = sb("w_te", [P, NB * NT, E])

        raw = sb("raw", [P, 2 * 2 * EC * P])
        w_raw = raw[:, 0:8 * D].rearrange("p (n d) -> p n d", d=D)
        ffn_raw = raw[:, 8 * D:16 * D].rearrange("p (w c q) -> p w c q", w=2, c=FC)
        wq, wk, wv, wo, bq, bk, bv, bo = ([None, None] for _ in range(8))
        for l in range(2):
            wq[l], wk[l], wv[l], wo[l] = (sb(f"w{n}{l}", [P, D]) for n in "qkvo")
            bq[l], bk[l] = (sb(f"b{n}{l}", [P, 1]) for n in "qk")
            bv[l], bo[l] = sb(f"bv{l}", [P, 1]), sb(f"bo{l}", [P, D])
        bv_wide = sb("bv_wide", [P, 2, P])
        w1T = sb("w1T", [P, FC, P])
        w2T = sb("w2T", [P, FC, D], BF16)
        conv_w = sb("conv_w", [P, FC, 3])
        conv_b = sb("conv_b", [P, FC])
        wq_stat = sb("wq_stat", [P, 8])
        router_raw = sb("router_raw", [E, D])
        routerT = sb("routerT", [P, E])
        fc_raw = raw[:, :].rearrange("p (r w f) -> p r w f", r=2, w=2)
        fc1_hi = sb("fc1_hi", [P, E, EC, P], F32R)
        fc1_lo = sb("fc1_lo", [P, E, EC, P], F32R)
        fc2_hi = sb("fc2_hi", [P, E, EC, D], F32R)

        q_stacks = sb("q_stacks", [P, 2, SETS, S], F32R)
        q_stack = [q_stacks[:, r, :, :] for r in range(2)]
        k_blocks = [sb(f"k_blocks{r}", [P, SETS, HPS, S], F32R) for r in range(2)]
        v_aug = [sb(f"v_aug{r}", [P, NT, H, HR]) for r in range(2)]
        ctx_in = sb("ctx_in", [P, NT, D])
        ctxT = [sb(f"ctxT{r}", [P, S]) for r in range(2)]
        qk_sum = sb("qk_sum", [P, 2, S])
        qk_parts = sb("qk_parts", [P, 6, S], F32R)
        row_max = sb("row_max", [P, NT, H])
        max_split = sb("max_split", [P, NT, 2, SETS // 2, 2, HPS], F32R)
        maxT = sb("maxT", [2 * HPS, 2, 2, S])
        probs = sb("probs", [P, 2, HPS, NT, S])
        o_raw = sb("o_raw", [P, SETS, S])
        rden = sb("rden", [P, NT, H])
        o_norm = sb("o_norm", [P, NT, D])
        o_normT = sb("o_normT", [P, S])
        mask_in = sb("mask_in", [P, NT, S], I32)
        mask_q = [sb(f"mask_q{r}", [P, NT, S]) for r in range(2)]
        mask_k = [sb(f"mask_k{r}", [P, NT, S], F32R) for r in range(2)]

        ln_st = sb("ln_st", [P, NB * NT, 6])
        ln_mv = sb("ln_mv", [P, NB * NT, 2])
        ln_ve = sb("ln_ve", [P, NB * NT])
        ln_rstd = sb("ln_rstd", [P, NB * NT])
        xn = sb("xn", [P, NT, D])
        qa = sb("qa", [P, NT, 3])
        NTT = NB * NT
        r_x = sb("r_x", [P, S])
        r_logit = sb("r_logit", [P, NTT, E])
        r_max = sb("r_max", [P, NTT])
        r_sum = sb("r_sum", [P, NTT])
        r_top = sb("r_top", [P, NTT, 8])
        r_idx = sb("r_idx", [P, NTT, 8], U32)
        r_idf = sb("r_idf", [P, NTT, 2])
        r_den = sb("r_den", [P, NTT])
        r_w = sb("r_w", [P, NTT, 2])
        r_pick = sb("r_pick", [P, 2, NTT, E])

        f_conv, f_act = (probs[:, 0, 2 * k:2 * k + 2, :, :].rearrange("p j k q -> p (j k q)")
                         .rearrange("p (c t) -> p c t", c=FC) for k in range(2))
        f_round = probs[:, 1, 0:2, :, :].rearrange("p j k q -> p (j k q)").rearrange("p (i h) -> p i h", i=NT)
        f_int = sb("f_int", [P, NT, FF], BF16)
        f_intT = sb("f_intT", [P, NT, FC, P], BF16)
        fa = sb("fa", [P, 4, NT])
        fa_last = sb("fa_last", [P, NT])

        GTP = GT * P
        fc2_lo = k_blocks[0][:, :, :, :].rearrange("p s j (e d) -> p (s j e) d", d=D).rearrange("p (e c) d -> p e c d", c=EC)
        h_act_sb, h_scaled_sb = (probs[:, k, :, :, :].rearrange("p c k q -> p c (k q)") for k in range(2))
        h_hi_sb, h_lo_sb = (k_blocks[1][:, 2 * k:2 * k + 2, :, :].rearrange("p s j q -> p (s j q)")
                            .rearrange("p (c t) -> p c t", c=EC) for k in range(2))
        w_parts = sb("w_parts", [P, NB * NT, 2, E], F32R)
        wT = q_stacks[:, :, :, :].rearrange("p r s (i t) -> p (r s i) t", t=P)
        pick = sb("pick", [P, E], F32R)
        yT = qk_sum[:, :, :].rearrange("p w q -> p (w q)")
        xn_all = probs[:, 0, :, :, :].rearrange("p j k q -> p (j k q)").rearrange("p (n d) -> p n d", d=D)

        q_dram = [nc.dram_tensor(f"q_dram{r}", (H, HR, S), F32).ap() for r in range(2)]
        k_dram = [nc.dram_tensor(f"k_dram{r}", (H, 3 * DH, S), F32).ap() for r in range(2)]

        held = sem("held")
        x_loaded = [sem("x_loaded0"), sem("x_loaded1")]
        w_loaded = sem("w_loaded")
        w1_loaded = sem("w1_loaded")
        ffn_loaded = sem("ffn_loaded")
        bias_loaded = sem("bias_loaded")
        fc_loaded = [sem("fc_loaded0"), sem("fc_loaded1")]
        zero_stored = sem("zero_stored")
        out_stored = sem("out_stored")
        const_ready = sem("const_ready")
        cast_ready = sem("cast_ready")
        stack_zeroed = sem("stack_zeroed")
        bias_ready, bo_ps, bo_new = sem("bias_ready"), sem("bo_ps"), sem("bo_new")
        x_biased = sem("x_biased")
        wT_ps, wT_sb = sem("wT_ps"), sem("wT_sb")
        f_stat, f_mean, f_tern = sem("f_stat"), sem("f_mean"), sem("f_tern")
        fc_ps, fc_hi, fc_done = sem("fc_ps"), sem("fc_hi"), sem("fc_done")

        class Ln:
            def __init__(self, n):
                self.st = sem(n + "_ln_stats")
                self.mv = sem(n + "_ln_mean_var")
                self.ve = sem(n + "_ln_var_eps")
                self.rstd = sem(n + "_ln_rstd")
                self.xn = sem(n + "_ln_xn")
                if n in ("a0", "f0"):
                    self.q = sem(n + "_ln_quant")
                self.xT = sem(n + "_ln_xT")
                if n != "a1":
                    self.xs = sem(n + "_ln_xT_sb")

        class Att:
            def __init__(self, n):
                s = lambda x: sem(n + "_" + x)
                self.ctx_in, self.cT_ps, self.cT_sb = s("ctx_in"), s("ctxT_ps"), s("ctxT_sb")
                self.qk_ps, self.qk_sum = s("qk_ps"), s("qk_sum")
                self.qk_hi, self.qk_lo = s("qk_hi"), s("qk_lo")
                self.to_dram = s("to_dram")
                self.stack = [s("stack_half0"), s("stack_half1")]
                self.v_ps, self.v_sb = s("v_ps"), s("v_sb")
                self.s_ps, self.s_max = s("s_ps"), s("s_max")
                self.m_hi, self.m_split = s("m_hi"), s("m_split")
                self.mT_ps, self.mT_sb = s("mT_ps"), s("mT_sb")
                self.m_in = [s("m_in_half0"), s("m_in_half1")]
                self.t_ps, self.p_sb = s("t_ps"), s("p_sb")
                self.pv = s("pv")
                self.o_sb = s("o_sb")
                self.oT_ps, self.rden, self.o_norm = s("oT_ps"), s("rden"), s("o_norm")
                self.nT_ps, self.nT_sb = s("nT_ps"), s("nT_sb")
                self.y_ps, self.x_new = s("y_ps"), s("x_new")
                if n == "a0":
                    return
                self.k_in, self.k_q = s("mask_in"), s("mask_q")
                self.kT_ps, self.kT_sb = s("maskT_ps"), s("maskT_sb")
                self.r_x, self.r_ps, self.r_log = s("router_x"), s("router_ps"), s("router_logits")
                self.x_hi, self.x_lo = s("x_hi"), s("x_lo")

        ln_pre, ln_a0, ln_f0, ln_a1 = Ln("pre"), Ln("a0"), Ln("f0"), Ln("a1")
        att = [Att("a0"), Att("a1")]
        fa_kept = sem("fa_kept")
        h_ps, h_tap, h_conv, h_act = sem("h_ps"), sem("h_tap"), sem("h_conv"), sem("h_act")
        g_ps, g_stat, g_round, g_int = sem("g_ps"), sem("g_stat"), sem("g_round"), sem("g_int")
        gi_ps, gi_sb, fy_ps, fx_new = sem("gi_ps"), sem("gi_sb"), sem("fy_ps"), sem("fx_new")
        route, r_exp = sem("route"), sem("router_exp")
        wT_zeroed = sem("wT_zeroed")
        w_split, wT_in_ps, wT_ready = sem("w_split"), sem("wT_in_ps"), sem("wT_ready")
        fc1_ps, w_ps = sem("fc1_ps"), sem("w_ps")
        h_silu, h_scaled, h_hi, h_used = sem("h_silu"), sem("h_scaled"), sem("h_hi"), sem("h_used")
        h_lo, h_lo_last = sem("h_lo"), sem("h_lo_last")
        y_sb, yT_ps, y_used = sem("y_sb"), sem("yT_ps"), sem("y_used")

        block = ctx.enter_context(nc.Block())

        def exists(b):
            return not isinstance(b, int) or 0 <= b < NB

        def after(b, k):
            return not isinstance(b, int) or b > k

        def bodies(eng, body, after_first=None):
            for b in range(-2, 2):
                body(b, b % 2)
                if b == -2 and after_first is not None:
                    after_first()
            with eng.Fori(1, NB // 2 - 1) as t:
                body(t * 2, 0)
                body(t * 2 + 1, 1)
            for b in range(NB - 2, NB + 2):
                body(b, b % 2)

        def ffn_steps(eng, step):
            for b in range(-1, 2):
                step(b, b % 2)
            with eng.Fori(1, NB // 2 - 1) as t:
                step(t * 2, 0)
                step(t * 2 + 1, 1)
            for b in range(NB - 2, NB + 1):
                step(b, b % 2)

        def hidden_ps(r, c):
            return ps[:, 2 * r + c // 2, c % 2 * S:c % 2 * S + S]

        def one(t, b):
            return t[:, bass.ds(b, 1)].rearrange("p o f -> p (o f)")

        def x_tiles(b):
            return x_res[:, bass.ds(b * NT, NT), :]

        def x_tile(b, i):
            return x_res[:, bass.ds(b * NT + i, 1), :].rearrange("p o d -> p (o d)")

        def hold(eng, semaphore, value):
            eng.wait_ge(semaphore, value)
            eng.sem_inc(held, 1)

        def minus_ones(eng, r):
            for j in range(HPS):
                last = eng.memset(k_blocks[r][j * HR:j * HR + 2, :, j, :].bitcast(F32), -1.0)
            last.then_inc(stack_zeroed, 1)

        def ln_stats(eng, s, b, produced):
            hold(eng, *produced)
            for i in range(NT):
                last = eng.bn_stats(ln_st[:, i, :], x_tile(b, i))
            last.then_inc(s.st, 1)
            hold(eng, s.st, b + 1)
            for i in range(NT):
                last = eng.bn_aggr(ln_mv[:, i, :], ln_st[:, i, :])
            last.then_inc(s.mv, 1)

        def ln_power(eng, s, b):
            hold(eng, s.mv, b + 1)
            eng.tensor_scalar(ln_ve[:, 0:NT], ln_mv[:, 0:NT, 1], LN_EPS, None, ALU.add).then_inc(s.ve, 1)
            eng.wait_ge(s.ve, b + 1)
            eng.tensor_tensor(ln_rstd[:, 0:NT], ln_ve[:, 0:NT], minus_half[:, 0:NT], ALU.pow).then_inc(s.rstd, 1)

        def ln_apply(eng, s, b, add_bias=None):
            eng.wait_ge(s.rstd, b + 1)
            eng.wait_ge(s.xT, b)
            for i in range(NT):
                last = eng.tensor_scalar(xn[:, i, :], x_tile(b, i), ln_mv[:, i, 0:1], ln_rstd[:, i:i + 1],
                                         ALU.subtract, ALU.mult)
            last.then_inc(s.xn, 1)
            if add_bias is not None:
                eng.wait_ge(s.xn, b + 1)
                eng.tensor_tensor(x_tiles(b), x_tiles(b),
                                  add_bias[:, None, :].to_broadcast([P, NT, D]), ALU.add).then_inc(s.q, 1)

        def quantise_rows(eng, s, b, part):
            if part == 0:
                eng.wait_ge(s.xn, b + 1)
                eng.tensor_reduce(qa[:, :, 0], xn[:, :, :], AX.X, ALU.max, apply_absolute_value=True).then_inc(s.q, 1)
                eng.wait_ge(s.q, b * 5 + 1)
                eng.tensor_scalar(qa[:, :, 1], qa[:, :, 0], QUANT_EPS, 1.0 / 127.0, ALU.max, ALU.mult).then_inc(s.q, 1)
            if part == 1:
                eng.wait_ge(s.q, b * 5 + 2)
                eng.reciprocal(qa[:, :, 2], qa[:, :, 1]).then_inc(s.q, 1)
                eng.wait_ge(s.q, b * 5 + 3)
                for i in range(NT):
                    last = eng.tensor_scalar(xn[:, i, :], xn[:, i, :], qa[:, i, 2:3], ROUND, ALU.mult, ALU.add)
                last.then_inc(s.q, 1)
            if part == 2:
                eng.wait_ge(s.q, b * 5 + 4)
                eng.tensor_scalar(xn[:, :, :], xn[:, :, :], ROUND + 127.0, ROUND - 128.0, ALU.min, ALU.max)
                eng.drain()
                for i in range(NT):
                    last = eng.tensor_scalar(xn[:, i, :], xn[:, i, :], ROUND, qa[:, i, 1:2], ALU.subtract, ALU.mult)
                last.then_inc(s.q, 1)

        def xn_transposes(eng, s, b, bank, col, ready):
            eng.wait_ge(*ready)
            for i in range(NT):
                last = eng.transpose(ps[:, bank, col + i * P:col + (i + 1) * P], xn[:, i, :], ident[:, :])
            last.then_inc(s.xT, 1)

        def stack_loads(eng, a, b, r, half):
            sets = slice(2 * half, 2 * half + 2)
            q_src = q_dram[r].rearrange("(s j) w q -> (j w) s q", j=HPS)
            eng.dma_start(q_stack[r][:, sets, :].bitcast(F32), q_src[:, sets, :]).then_inc(a.stack[half], DMA)
            for j in range(HPS):
                k_src = k_dram[r].rearrange("(s j) w q -> j w s q", j=HPS)[j]
                eng.dma_start(k_blocks[r][j * HR + DH:(j + 1) * HR, sets, j, :].bitcast(F32),
                              k_src[:, sets, :]).then_inc(a.stack[half], DMA)

        def max_loads(eng, a, b, r, half):
            eng.wait_ge(a.mT_sb, b * 2 + half + 1)
            for part in range(2):
                eng.dma_start(q_stack[r][part:part + (HPS - 1) * HR + 1:HR, 2 * half:2 * half + 2, :].bitcast(F32),
                              maxT[part * HPS:(part + 1) * HPS, half, :, :]).then_inc(a.m_in[half], DMA)

        def context_load(eng, a, b):
            eng.dma_start(ctx_in[:, :, :], inp["ctx_1024"][bass.ds(b, 1)].rearrange("o (i p) d -> p (o i) d", p=P)
                          ).then_inc(a.ctx_in, DMA)

        def mask_load(eng, a, b):
            m_src = inp["mask_Bx1xSxS2_ik1"][bass.ds(b, 1)]
            eng.dma_start(mask_in[:, :, :], m_src.rearrange("o u (i p) k -> p (o u i) k", p=P)).then_inc(a.k_in, DMA)

        def attention_sync(eng, l):
            a = att[l]

            def body(b, r):
                if exists(b + 2) and (l == 1 or after(b, -2)):
                    if after(b, -2):
                        eng.wait_ge(a.cT_ps, b + 2)
                    else:
                        eng.wait_ge(att[0].cT_ps, NB)
                    context_load(eng, a, b + 2)
                    if l == 1:
                        if after(b, -2):
                            eng.wait_ge(a.k_q, b + 2)
                        mask_load(eng, a, b + 2)
                if exists(b + 1):
                    if exists(b - 1):
                        eng.wait_ge(a.t_ps, b * 16)
                    stack_loads(eng, a, b + 1, 1 - r, 1)
                if exists(b):
                    max_loads(eng, a, b, r, 1)
                if exists(b + 2):
                    eng.wait_ge(a.qk_lo, b + 3)
                    if after(b, -1):
                        for half in range(2):
                            eng.wait_ge(a.stack[half], (b + 1) * 5 * DMA)
                    elif l == 1:
                        for half in range(2):
                            eng.wait_ge(att[0].stack[half], NB * 5 * DMA)
                    eng.dma_start(q_dram[r][:, DH:HR, :].rearrange("h w q -> h (w q)"),
                                  qk_parts[:, 0:3, :].bitcast(F32).rearrange("p t q -> p (t q)")).then_inc(a.to_dram, DMA)
                    eng.dma_start(k_dram[r][:, :, :].rearrange("h w q -> h (w q)"),
                                  qk_parts[:, 3:6, :].bitcast(F32).rearrange("p t q -> p (t q)")).then_inc(a.to_dram, DMA)
                    hold(eng, a.to_dram, (b + 3) * 2 * DMA)
                    if exists(b):
                        eng.wait_ge(a.t_ps, b * 16 + 8)
                    else:
                        if l == 0:
                            eng.wait_ge(stack_zeroed, 2)
                            eng.wait_ge(zero_stored, 2 * DMA)
                        else:
                            eng.wait_ge(att[0].t_ps, NB * 16)
                    stack_loads(eng, a, b + 2, r, 0)
                if exists(b + 1):
                    max_loads(eng, a, b + 1, 1 - r, 0)

            bodies(eng, body)

        @block.sync
        def _(eng):
            x_src = inp["x"].rearrange("b (i p) d -> p (b i) d", p=P)

            def x_load(half):
                t = slice(half * NB * NT // 2, (half + 1) * NB * NT // 2)
                eng.dma_start(x_res[:, t, :], x_src[:, t, :]).then_inc(x_loaded[half], DMA)

            x_load(0)
            for n, w in enumerate("qkvo"):
                eng.dma_start(w_raw[:, n, :], inp[f"L0_xattn_W{w}"]).then_inc(w_loaded, DMA)
            context_load(eng, att[0], 0)
            x_load(1)
            for l in range(2):
                eng.dma_start(bq[l][:, :], inp[f"L{l}_xattn_bq"].rearrange("(p o) -> p o", o=1)).then_inc(bias_loaded, DMA)
                eng.dma_start(bk[l][:, :], inp[f"L{l}_xattn_bk"].rearrange("(p o) -> p o", o=1)).then_inc(bias_loaded, DMA)
                eng.dma_start(bv[l][:, :], inp[f"L{l}_xattn_bv"].rearrange("(p o) -> p o", o=1)).then_inc(bias_loaded, DMA)
                eng.dma_start(bo[l][:, :], inp[f"L{l}_xattn_bo"].partition_broadcast(P)).then_inc(bias_loaded, DMA)
            eng.wait_ge(const_ready, 2)
            for r in range(2):
                eng.dma_start(q_dram[r][:, 0:DH, :], zeros[:, :]).then_inc(zero_stored, DMA)
            for n, dst in enumerate((w_raw[:, 4, :], wk[1][:, :], wv[1][:, :], wo[1][:, :])):
                eng.dma_start(dst, inp[f"L1_xattn_W{'qkvo'[n]}"]).then_inc(w1_loaded, DMA)
            eng.dma_start(ffn_raw[:, 0, :, :], inp["L0_ffn_w1"].rearrange("(c p) d -> p c d", p=P)).then_inc(ffn_loaded, DMA)
            eng.dma_start(ffn_raw[:, 1, :, :], inp["L0_ffn_w2"].rearrange("d (c p) -> d c p", p=P)).then_inc(ffn_loaded, DMA)
            eng.dma_start(conv_w[:, :, :], inp["L0_ffn_conv_w"].rearrange("(c p) o k -> p (c o) k", p=P)).then_inc(ffn_loaded, DMA)
            eng.dma_start(conv_b[:, :], inp["L0_ffn_conv_b"].rearrange("(c p) -> p c", p=P),
                          allow_slow_non_contiguous=True).then_inc(ffn_loaded, DMA)
            eng.dma_start(router_raw[:, :], inp["L1_ffn_router_w"]).then_inc(ffn_loaded, DMA)
            attention_sync(eng, 0)
            if stages >= 3:
                attention_sync(eng, 1)
            if stages >= 4:
                for e in range(E):
                    if e >= 2:
                        eng.wait_ge(fc_ps, (e - 1) * 2)
                    eng.dma_start(fc_raw[:, e % 2, 0, :].rearrange("p (c d) -> p c d", c=EC),
                                  inp["L1_ffn_fc1_w"][e].rearrange("(c p) d -> p c d", p=P)).then_inc(fc_loaded[e % 2], DMA)
                    eng.dma_start(fc_raw[:, e % 2, 1, :], inp["L1_ffn_fc2_w"][e]).then_inc(fc_loaded[e % 2], DMA)
                with eng.Fori(0, NG) as g:
                    hold(eng, y_used, g + 1)
                    dst = out.rearrange("b (i p) d -> p (b i) d", p=P)
                    eng.dma_start(dst[:, bass.ds(g * GT, GT), :], x_res[:, bass.ds(g * GT, GT), :]).then_inc(out_stored, DMA)
                eng.wait_ge(out_stored, NG * DMA)
            else:
                if stages == 1:
                    eng.wait_ge(ln_a0.xn, NB)
                elif stages == 2:
                    eng.wait_ge(ln_f0.xn, NB)
                    eng.wait_ge(ln_f0.q, NB)
                else:
                    eng.wait_ge(att[1].x_new, NB)
                eng.dma_start(out.rearrange("b (i p) d -> p (b i) d", p=P), x_res[:, :, :]).then_inc(out_stored, DMA)
                eng.wait_ge(out_stored, DMA)

        def attention_gpsimd(eng, l, after_first=None):
            a = att[l]
            s = (ln_a0, ln_a1)[l]

            def body(b, r):
                if l == 1 and exists(b - 2):
                    eng.wait_ge(a.x_hi, b - 1)
                    eng.tensor_tensor(one(xlT_all, b - 2), r_x[:, :], one(xhT_all, b - 2).bitcast(F32),
                                      ALU.subtract).then_inc(a.x_lo, 1)
                if l == 1 and exists(b + 2):
                    hold(eng, a.k_in, (b + 3) * DMA)
                    if exists(b):
                        hold(eng, a.s_max, (b + 1) * 16)
                        hold(eng, a.kT_ps, b + 1)
                    eng.tensor_scalar(mask_q[r][:, :, :], mask_in[:, :, :], -MASK_A * MASK_B, 1.0,
                                      ALU.mult, ALU.mult).then_inc(a.k_q, 1)
                if exists(b + 2):
                    eng.wait_ge(a.qk_hi, b + 3)
                    eng.tensor_tensor(qk_parts[:, 2:4, :], qk_sum[:, :, :], qk_parts[:, 1:5:3, :].bitcast(F32),
                                      ALU.subtract).then_inc(a.qk_lo, 1)
                if exists(b + 1):
                    max_parts(b + 1, 0)
                if exists(b - 1):
                    ln_power(eng, s, b - 1)
                if exists(b + 1):
                    max_parts(b + 1, 1)

            def max_parts(b, half):
                if after(b, 0):
                    eng.wait_ge(a.mT_ps, b * 2)
                hold(eng, a.s_max, b * 16 + half * 8 + 8)
                src = row_max[:, :, half * 8:half * 8 + 8].rearrange("p i (s j) -> p i s j", j=HPS)
                hi, lo = (max_split[:, :, half, :, part, :] for part in range(2))
                eng.tensor_scalar(hi, src, 1.0, 1.0, ALU.mult, ALU.mult).then_inc(a.m_hi, 1)
                eng.wait_ge(a.m_hi, b * 2 + half + 1)
                eng.tensor_tensor(lo, src, hi.bitcast(F32), ALU.subtract).then_inc(a.m_split, 1)

            bodies(eng, body, after_first)

        @block.gpsimd
        def _(eng):
            eng.memset(ident[:, :], 0.0).then_inc(const_ready, 1)
            eng.memset(zeros[:, :], 0.0).then_inc(const_ready, 1)
            eng.wait_ge(const_ready, 1)
            eng.affine_select(out=ident[:, :], in_=ident[:, :], compare_op=ALU.not_equal, fill=1.0, base=0,
                              pattern=[[-1, P]], channel_multiplier=1).then_inc(const_ready, 1)
            eng.memset(minus_half[:, :], -0.5).then_inc(const_ready, 1)
            eng.memset(k_blocks[1][:, :, :, :].bitcast(F32), 0.0).then_inc(cast_ready, 1)
            eng.memset(mean_ones[:, :], 1.0 / (FF * D)).then_inc(const_ready, 1)
            for e in range(E):
                last = eng.memset(iota_e[:, e:e + 1], float(e))
            last.then_inc(const_ready, 1)
            for r in range(2):
                eng.memset(v_aug[r][:, :, :, :], 1.0).then_inc(const_ready, 1)
            eng.wait_ge(const_ready, 8)
            for half in range(2):
                t = slice(half * NB * NT // 2, (half + 1) * NB * NT // 2)
                eng.wait_ge(ln_pre.mv, half + 1)
                eng.tensor_scalar(ln_ve[:, t], ln_mv[:, t, 1], LN_EPS, None, ALU.add).then_inc(ln_pre.ve, 1)
                eng.wait_ge(ln_pre.ve, half + 1)
                eng.tensor_tensor(ln_rstd[:, t], ln_ve[:, t], minus_half[:, t], ALU.pow).then_inc(ln_pre.rstd, 1)

            def add_output_bias():
                eng.wait_ge(ln_pre.xn, 2)
                eng.wait_ge(bo_new, 2)
                eng.tensor_tensor(x_res[:, :, :], x_res[:, :, :],
                                  bo[0][:, None, :].to_broadcast([P, NB * NT, D]), ALU.add).then_inc(x_biased, 1)

            attention_gpsimd(eng, 0, add_output_bias)
            if stages >= 2:
                with eng.Fori(0, NB) as b:
                    ln_power(eng, ln_f0, b)
            if stages >= 3:
                attention_gpsimd(eng, 1)
            if stages >= 4:
                eng.wait_ge(att[1].t_ps, NB * 16)
                eng.memset(wT[:, :, :].bitcast(F32), 0.0).then_inc(wT_zeroed, 1)

                def low_last(g, e):
                    u = g * E + e
                    eng.wait_ge(h_hi, u * EC + EC)
                    if e > 0 or after(g, 0):
                        eng.wait_ge(h_used, u * EC)
                    eng.tensor_tensor(h_lo_sb[:, EC - 1, :], h_scaled_sb[:, EC - 1, :], h_hi_sb[:, EC - 1, :].bitcast(F32),
                                      ALU.subtract).then_inc(h_lo_last, 1)

                for e in range(E):
                    low_last(0, e)
                with eng.Fori(1, NG) as g:
                    for e in range(E):
                        low_last(g, e)

        def attention_scalar(eng, l, after_first=None):
            a, at = att[l], AT[l]
            s = (ln_a0, ln_a1)[l]

            def body(b, r):
                for n in range(H):
                    if exists(b):
                        eng.wait_ge(a.t_ps, b * 16 + n + 1)
                        if n % HPS == 0 and (n >= 8 or after(b, 0)):
                            eng.wait_ge(a.pv, b * 4 + n // HPS - 1)
                        eng.activation(probs[:, n // HPS % 2, n % HPS, :, :].rearrange("p k q -> p (k q)"),
                                       ps[:, BANK_T[n % 3], :], ACT.Exp).then_inc(a.p_sb, 1)
                    if l == 0 and n == 0 and exists(b - 2):
                        eng.wait_ge(s.xT, b - 1)
                        eng.activation(one(xnT_all, b - 2), ps[:, BANK_M, 0:S], ACT.Copy).then_inc(s.xs, 1)
                    if l == 1 and n == 0 and exists(b - 2):
                        eng.wait_ge(a.r_ps, b - 1)
                        eng.activation(r_logit[:, bass.ds((b - 2) * NT, NT), :].rearrange("p i e -> p (i e)"),
                                       ps[:, BANK_M, 0:NT * E], ACT.Copy).then_inc(a.r_log, 1)
                    if n == at["a_ctx"] and exists(b + 2):
                        eng.wait_ge(a.cT_ps, b + 3)
                        eng.activation(ctxT[r][:, :], ps[:, BANK_M, 0:S], ACT.Copy).then_inc(a.cT_sb, 1)
                    if n == at["a_max1"] and exists(b):
                        max_copy(b, 1)
                    if n == at["a_out1"] and exists(b - 1):
                        out_copy(b - 1, 1)
                    if n == at["a_norm"] and exists(b - 1):
                        eng.wait_ge(a.nT_ps, b)
                        eng.activation(o_normT[:, :], ps[:, BANK_O[1], 0:S], ACT.Copy).then_inc(a.nT_sb, 1)
                    if n == at["a_v"] and exists(b + 1):
                        eng.wait_ge(a.v_ps, b + 2)
                        if exists(b - 1):
                            eng.wait_ge(a.pv, b * 4)
                        elif l == 1:
                            eng.wait_ge(att[0].pv, NB * 4)
                        eng.activation(v_aug[1 - r][:, :, :, 0:DH],
                                       ps[:, BANK_M, 0:NT * D].rearrange("p (i h d) -> p i h d", i=NT, d=DH),
                                       ACT.Copy).then_inc(a.v_sb, 1)
                    if n == at["a_qk"] and exists(b + 2):
                        eng.wait_ge(a.qk_ps, b + 3)
                        if after(b, -2):
                            eng.wait_ge(a.qk_lo, b + 2)
                        elif l == 0:
                            eng.wait_ge(bias_ready, 2)
                        eng.activation(qk_sum[:, 0, :], ps[:, BANK_M, 0:S], ACT.Identity, bias=bq[l][:, 0:1])
                        eng.activation(qk_sum[:, 1, :], ps[:, BANK_M, S:2 * S], ACT.Identity,
                                       bias=bk[l][:, 0:1]).then_inc(a.qk_sum, 1)
                    if n == at["a_q_hi"] and exists(b + 2):
                        eng.wait_ge(a.qk_sum, b + 3)
                        if after(b, -2):
                            eng.wait_ge(a.to_dram, (b + 2) * 2 * DMA)
                        high_part(0)
                    if n == at["a_k_hi"] and exists(b + 2):
                        high_part(1).then_inc(a.qk_hi, 1)
                    if n == at["a_out0"] and exists(b):
                        out_copy(b, 0)
                    if n == at["a_max0"] and exists(b + 1):
                        max_copy(b + 1, 0)
                    if l == 1 and n == at["a_mask"] and exists(b + 1):
                        eng.wait_ge(a.kT_ps, b + 2)
                        eng.activation(mask_k[1 - r][:, :, :].rearrange("p k q -> p (k q)"), ps[:, BANK_M, :],
                                       ACT.Copy, scale=-1.0 / MASK_A).then_inc(a.kT_sb, 1)
                    if l == 1 and n == 15 and exists(b - 1):
                        eng.wait_ge(s.xT, b)
                        eng.wait_ge(a.x_lo, b - 1)
                        eng.activation(r_x[:, :], ps[:, BANK_M, 0:S], ACT.Copy).then_inc(a.r_x, 1)
                        eng.activation(one(xhT_all, b - 1), ps[:, BANK_M, 0:S], ACT.Copy).then_inc(a.x_hi, 1)

            def high_part(w):
                return eng.activation(qk_parts[:, 4 * w:4 * w + 2, :], qk_sum[:, w, None, :].to_broadcast([P, 2, S]), ACT.Copy)

            def max_copy(b, half):
                eng.wait_ge(a.mT_ps, b * 2 + half + 1)
                if after(b, 0):
                    eng.wait_ge(a.m_in[half], b * 2 * DMA)
                elif l == 1:
                    eng.wait_ge(att[0].m_in[half], NB * 2 * DMA)
                bank = (BANK_M, BANK_O[0])[half]
                eng.activation(maxT[:, half, :, :].rearrange("p s q -> p (s q)"), ps[0:2 * HPS, bank, :],
                               ACT.Copy).then_inc(a.mT_sb, 1)

            def out_copy(b, half):
                eng.wait_ge(a.pv, b * 4 + 2 * half + 2)
                if after(b, 0):
                    eng.wait_ge(a.oT_ps, b * 2)
                eng.activation(o_raw[:, 2 * half:2 * half + 2, :].rearrange("p s q -> p (s q)"),
                               ps[:, BANK_O[half], :], ACT.Copy).then_inc(a.o_sb, 1)

            bodies(eng, body, after_first)

        def ffn_scalar(eng):
            def taps(b, r):
                for c in range(FC):
                    eng.wait_ge(h_ps, b * 2 + c // 2 + 1)
                    if c == 0:
                        eng.wait_ge(h_act, b)
                    eng.activation(f_conv[:, c, :], hidden_ps(r, c), ACT.Identity, scale=conv_w[:, c, 1:2],
                                   bias=conv_b[:, c:c + 1]).then_inc(h_tap, 1)

            def silu(b):
                eng.wait_ge(h_conv, b * 2 * FC + 2 * FC)
                eng.wait_ge(g_ps, b * NT)
                eng.activation(f_act[:, :, :].rearrange("p c t -> p (c t)"),
                               f_conv[:, :, :].rearrange("p c t -> p (c t)"), ACT.Silu).then_inc(h_act, 1)

            def rounding(b):
                eng.wait_ge(g_stat, b * 5 + 5)
                eng.wait_ge(g_int, b * 2 * NT)
                for i in range(NT):
                    eng.activation(f_round[:, i, :], ps[:, 4 + i, :], ACT.Copy, scale=fa[:, 1, i:i + 1],
                                   bias=ROUND).then_inc(g_round, 1)

            def int_copy(b):
                for i in range(NT):
                    eng.wait_ge(gi_ps, b * NT + i + 1)
                    eng.wait_ge(fy_ps, b)
                    eng.activation(f_intT[:, i, :, :].rearrange("p c t -> p (c t)"),
                                   ps[:, 6, i * 256:(i + 1) * 256].bitcast(BF16), ACT.Copy).then_inc(gi_sb, 1)

            def xT_copy(b):
                eng.wait_ge(ln_f0.xT, b + 1)
                eng.activation(one(xnT_all, b), ps[:, 7, S:2 * S], ACT.Copy).then_inc(ln_f0.xs, 1)

            def step(b, r):
                if exists(b + 1):
                    taps(b + 1, 1 - r)
                if exists(b - 1):
                    int_copy(b - 1)
                if exists(b - 2):
                    xT_copy(b - 2)
                if exists(b):
                    rounding(b)
                if exists(b + 1):
                    silu(b + 1)

            ffn_steps(eng, step)
            xT_copy(NB - 1)

        @block.scalar
        def _(eng):
            eng.wait_ge(wT_ps, 1)
            eng.activation(wq[0][:, :], ps[:, BANK_M, 0:D], ACT.Copy, scale=QSCALE)
            for n, w in enumerate((wk, wv, wo)):
                last = eng.activation(w[0][:, :], ps[:, BANK_M, (n + 1) * D:(n + 2) * D], ACT.Copy)
            last.then_inc(wT_sb, 1)
            eng.wait_ge(bias_loaded, 8 * DMA)
            for l in range(2):
                eng.activation(bq[l][:, :], bq[l][:, :], ACT.Copy, scale=QSCALE).then_inc(bias_ready, 1)
            eng.wait_ge(const_ready, 2)
            for l in range(2):
                eng.activation(bv_wide[:, l, :], zeros[:, 0:P], ACT.Identity, bias=bv[l][:, 0:1]).then_inc(bias_ready, 1)

            def pre_copies(half):
                for g in range(half * NB // 4, (half + 1) * NB // 4):
                    eng.wait_ge(ln_pre.xT, g + 1)
                    eng.activation(xnT_all[:, 2 * g:2 * g + 2, :].rearrange("p b t -> p (b t)"), ps[:, g, :],
                                   ACT.Copy).then_inc(ln_pre.xs, 1)

            def second_half():
                pre_copies(1)
                eng.wait_ge(w1_loaded, 4 * DMA)
                eng.activation(wq[1][:, :], w_raw[:, 4, :], ACT.Copy, scale=QSCALE).then_inc(wT_sb, 1)

            pre_copies(0)
            attention_scalar(eng, 0, second_half)
            if stages >= 2:
                for c in range(FC // 2):
                    eng.wait_ge(wT_ps, c + 2)
                eng.activation(w1T[:, :, :].rearrange("p c h -> p (c h)"), ps[:, 0, :], ACT.Copy).then_inc(wT_sb, 1)
                eng.activation(w2T[:, :, :].rearrange("p c h -> p (c h)"), ps[:, 1, :], ACT.Copy).then_inc(wT_sb, 1)
                eng.wait_ge(wT_ps, 4)
                eng.activation(routerT[:, :], ps[:, 2, 0:E], ACT.Copy).then_inc(wT_sb, 1)
                eng.wait_ge(f_tern, 8)
                ffn_scalar(eng)
            if stages >= 3:
                attention_scalar(eng, 1)
            if stages >= 4:
                for e in range(E):
                    for w, part in enumerate((fc1_hi, fc2_hi)):
                        eng.wait_ge(fc_ps, 2 * e + w + 1)
                        eng.activation(part[:, e, :, :].rearrange("p c h -> p (c h)"), ps[:, e % 3 * 2 + w, :],
                                       ACT.Copy).then_inc(fc_hi, 1)
                eng.wait_ge(route, 2)
                eng.activation(r_logit[:, :, :], r_logit[:, :, :], ACT.Exp).then_inc(r_exp, 1)
                eng.wait_ge(wT_zeroed, 1)
                for g in range(NG):
                    eng.wait_ge(wT_in_ps, g + 1)
                    eng.activation(wT[0:2 * E, g * GT:(g + 1) * GT, :].rearrange("p i t -> p (i t)"),
                                   ps[0:2 * E, 4 + g, :], ACT.Copy).then_inc(wT_ready, 1)

                def silu(g, e, c):
                    k = (g * E + e) * EC + c
                    eng.wait_ge(fc1_ps, k + 1)
                    if e > 0 or after(g, 0):
                        eng.wait_ge(h_scaled, k + 1 - EC)
                    eng.activation(h_act_sb[:, c, :], ps[:, c, :], ACT.Silu).then_inc(h_silu, 1)

                def high(g, e, c):
                    k = (g * E + e) * EC + c
                    eng.wait_ge(h_scaled, k + 1)
                    if e > 0 or after(g, 0):
                        eng.wait_ge(h_used, k + 1 - EC)
                    eng.activation(h_hi_sb[:, c, :], h_scaled_sb[:, c, :], ACT.Copy).then_inc(h_hi, 1)

                def group(g):
                    for e in range(E):
                        for c in range(EC):
                            silu(g, e, c)
                            if c > 0:
                                high(g, e, c - 1)
                            elif e > 0:
                                high(g, e - 1, EC - 1)
                            elif after(g, 0):
                                high(g - 1, E - 1, EC - 1)
                        if e == 0 and after(g, 0):
                            group_output(g - 1)

                def group_output(g):
                    eng.wait_ge(h_used, (g * E + E) * EC)
                    eng.wait_ge(yT_ps, g)
                    eng.activation(yT[:, :], ps[:, 6, :], ACT.Copy).then_inc(y_sb, 1)

                group(0)
                with eng.Fori(1, NG) as g:
                    group(g)
                high(NG - 1, E - 1, EC - 1)
                group_output(NG - 1)

        def attention_vector(eng, l):
            a, at = att[l], AT[l]
            s = (ln_a0, ln_a1)[l]

            def body(b, r):
                for n in range(H):
                    if exists(b + 1):
                        if l == 0:
                            eng.wait_ge(a.s_ps, (b + 1) * 16 + n + 1)
                            eng.tensor_reduce(row_max[:, :, n], ps[:, BANK_S[n % 2], :].rearrange("p (i k) -> p i k", i=NT),
                                              AX.X, ALU.max).then_inc(a.s_max, 1)
                        else:
                            hold(eng, a.s_ps, (b + 1) * 16 + n + 1)
                            for i in range(NT):
                                scored = ps[:, BANK_S[n % 2], i * S:(i + 1) * S]
                                last = eng.tensor_tensor_reduce(
                                    out=scored, in0=scored,
                                    in1=mask_q[1 - r][:, i, :], scale=1.0, scalar=-3.0e38, op0=ALU.add, op1=ALU.max,
                                    accum_out=row_max[:, i, n:n + 1])
                            last.then_inc(a.s_max, 1)
                    if n == at["d_norm"] and exists(b - 1):
                        t = b - 1
                        o_view = [ps[:, BANK_O[1 - i], :].rearrange("p (h r) -> p h r", r=HR) for i in range(NT)]
                        for i in range(NT):
                            eng.wait_ge(a.oT_ps, t * 2 + i + 1)
                            eng.reciprocal(rden[:, i, :], o_view[i][:, :, DH]).then_inc(a.rden, 1)
                        eng.wait_ge(a.nT_ps, t)
                        for i in range(NT):
                            eng.wait_ge(a.rden, t * 2 + i + 1)
                            eng.tensor_tensor(o_norm[:, i, :].rearrange("p (h d) -> p h d", d=DH), o_view[i][:, :, 0:DH],
                                              rden[:, i, :, None].to_broadcast([P, H, DH]), ALU.mult).then_inc(a.o_norm, 1)
                    if n == at["d_res"] and exists(b - 1):
                        eng.wait_ge(a.y_ps, b)
                        if l == 0:
                            eng.wait_ge(x_biased, 1)
                        else:
                            eng.wait_ge(ln_f0.q, b)
                        eng.tensor_tensor(x_tiles(b - 1), ps[:, BANK_O[1], S:2 * S].rearrange("p (i d) -> p i d", i=NT),
                                          x_tiles(b - 1), ALU.add).then_inc(a.x_new, 1)
                        ln_stats(eng, s, b - 1, (a.x_new, b))
                    if n == at["d_ln"] and exists(b - 1):
                        ln_apply(eng, s, b - 1)
                    if l == 0 and n in at["d_quant"] and exists(b - 1):
                        quantise_rows(eng, s, b - 1, at["d_quant"].index(n))

            bodies(eng, body)

        def routing(eng):
            eng.wait_ge(att[1].r_log, NB)
            eng.tensor_reduce(r_max[:, :], r_logit[:, :, :], AX.X, ALU.max).then_inc(route, 1)
            eng.wait_ge(route, 1)
            eng.tensor_tensor(r_logit[:, :, :], r_logit[:, :, :], r_max[:, :, None].to_broadcast([P, NTT, E]),
                              ALU.subtract).then_inc(route, 1)
            eng.wait_ge(r_exp, 1)
            eng.tensor_reduce(r_sum[:, :], r_logit[:, :, :], AX.X, ALU.add).then_inc(route, 1)
            eng.wait_ge(route, 3)
            eng.reciprocal(r_sum[:, :], r_sum[:, :]).then_inc(route, 1)
            eng.wait_ge(route, 4)
            eng.tensor_tensor(r_logit[:, :, :], r_logit[:, :, :], r_sum[:, :, None].to_broadcast([P, NTT, E]),
                              ALU.mult).then_inc(route, 1)
            eng.wait_ge(route, 5)
            for i in range(NTT):
                last = eng.max(r_top[:, i, :], r_logit[:, i, :])
            last.then_inc(route, 1)
            eng.wait_ge(route, 6)
            for i in range(NTT):
                eng.max_index(r_idx[:, i, :], r_top[:, i, :], r_logit[:, i, :])
            eng.tensor_tensor(r_den[:, :], r_top[:, :, 0], r_top[:, :, 1], ALU.add).then_inc(route, 1)
            eng.wait_ge(route, 7)
            eng.tensor_scalar(r_den[:, :], r_den[:, :], 1e-9, None, ALU.max).then_inc(route, 1)
            eng.tensor_copy(r_idf[:, :, :], r_idx[:, :, 0:2])
            eng.wait_ge(route, 8)
            eng.reciprocal(r_den[:, :], r_den[:, :]).then_inc(route, 1)
            eng.wait_ge(route, 9)
            eng.tensor_tensor(r_w[:, :, :], r_top[:, :, 0:2], r_den[:, :, None].to_broadcast([P, NTT, 2]),
                              ALU.mult).then_inc(route, 1)
            eng.wait_ge(route, 10)
            for k in range(2):
                last = eng.tensor_tensor(r_pick[:, k, :, :], iota_e[:, None, :].to_broadcast([P, NTT, E]),
                                         r_idf[:, :, k:k + 1].to_broadcast([P, NTT, E]), ALU.is_equal)
            last.then_inc(route, 1)
            eng.wait_ge(route, 11)
            for k in range(2):
                last = eng.tensor_tensor(r_pick[:, k, :, :], r_pick[:, k, :, :],
                                         r_w[:, :, k:k + 1].to_broadcast([P, NTT, E]), ALU.mult)
            last.then_inc(route, 1)
            eng.wait_ge(route, 12)
            eng.tensor_tensor(w_te[:, :, :], r_pick[:, 0, :, :], r_pick[:, 1, :, :], ALU.add).then_inc(route, 1)
            hold(eng, route, 13)

        def ffn_vector(eng):
            def conv(b, r):
                for c in range(FC):
                    eng.wait_ge(h_tap, b * FC + c // 2 * 2 + 2)
                    eng.scalar_tensor_tensor(out=f_conv[:, c, 1:S], in0=hidden_ps(r, c)[:, 0:S - 1], scalar=conv_w[:, c, 0:1],
                                             in1=f_conv[:, c, 1:S], op0=ALU.mult, op1=ALU.add).then_inc(h_conv, 1)
                for c in range(FC):
                    eng.wait_ge(h_conv, b * 2 * FC + c + 1)
                    eng.scalar_tensor_tensor(out=f_conv[:, c, 0:S - 1], in0=hidden_ps(r, c)[:, 1:S], scalar=conv_w[:, c, 2:3],
                                             in1=f_conv[:, c, 0:S - 1], op0=ALU.mult, op1=ALU.add).then_inc(h_conv, 1)

            def keep_factors(b):
                if after(b, 0):
                    eng.wait_ge(fx_new, b)
                eng.wait_ge(g_stat, b * 5 + 5)
                eng.tensor_copy(fa_last[:, :], fa[:, 2, :]).then_inc(fa_kept, 1)

            def quant_scale(b):
                for i in range(NT):
                    eng.wait_ge(g_ps, b * NT + i + 1)
                    last = eng.tensor_reduce(fa[:, 0, i:i + 1], ps[:, 4 + i, :], AX.X, ALU.max, apply_absolute_value=True)
                    last.then_inc(g_stat, 1)
                eng.wait_ge(g_stat, b * 5 + 2)
                if after(b, 0):
                    eng.wait_ge(g_round, b * NT)
                eng.tensor_scalar(fa[:, 3, :], fa[:, 0, :], QUANT_EPS, 1.0 / 127.0, ALU.max, ALU.mult).then_inc(g_stat, 1)
                eng.wait_ge(g_stat, b * 5 + 3)
                if after(b, 0):
                    eng.wait_ge(fa_kept, b)
                eng.reciprocal(fa[:, 1, :], fa[:, 3, :]).then_inc(g_stat, 1)
                eng.tensor_scalar(fa[:, 2, :], fa[:, 3, :], wq_stat[:, 3:4], None, ALU.mult).then_inc(g_stat, 1)

            def quant_clip(b):
                for i in range(NT):
                    eng.wait_ge(g_round, b * NT + i + 1)
                    eng.wait_ge(gi_ps, b * NT)
                    eng.tensor_scalar(f_round[:, i, :], f_round[:, i, :], ROUND, 127.0, ALU.subtract,
                                      ALU.min).then_inc(g_int, 1)
                for i in range(NT):
                    eng.wait_ge(g_int, b * 2 * NT + i + 1)
                    eng.tensor_scalar(f_int[:, i, :], f_round[:, i, :], -128.0, None, ALU.max).then_inc(g_int, 1)

            def residual(b):
                eng.wait_ge(fy_ps, b + 1)
                eng.wait_ge(fa_kept, b + 1)
                for i in range(NT):
                    last = eng.scalar_tensor_tensor(out=x_tile(b, i), in0=ps[:, 7, i * P:(i + 1) * P],
                                                    scalar=fa_last[:, i:i + 1], in1=x_tile(b, i), op0=ALU.mult, op1=ALU.add)
                last.then_inc(fx_new, 1)
                ln_stats(eng, ln_f0, b, (fx_new, b + 1))

            def step(b, r):
                if exists(b - 1):
                    keep_factors(b - 1)
                if exists(b):
                    quant_scale(b)
                if exists(b + 1):
                    conv(b + 1, 1 - r)
                if exists(b - 1):
                    residual(b - 1)
                if exists(b):
                    quant_clip(b)
                if exists(b - 1):
                    ln_apply(eng, ln_f0, b - 1, bo[1])

            ffn_steps(eng, step)

        @block.vector
        def _(eng):
            eng.memset(k_blocks[0][:, :, :, :].bitcast(F32), 0.0).then_inc(cast_ready, 1)

            def pre_stats(half):
                tiles = range(half * NB * NT // 2, (half + 1) * NB * NT // 2)
                eng.wait_ge(x_loaded[half], DMA)
                for n in tiles:
                    last = eng.bn_stats(ln_st[:, n, :], x_res[:, n, :])
                last.then_inc(ln_pre.st, 1)
                eng.wait_ge(ln_pre.st, half + 1)
                for n in tiles:
                    last = eng.bn_aggr(ln_mv[:, n, :], ln_st[:, n, :])
                last.then_inc(ln_pre.mv, 1)

            def pre_apply(half):
                eng.wait_ge(ln_pre.rstd, half + 1)
                for n in range(half * NB * NT // 2, (half + 1) * NB * NT // 2):
                    last = eng.tensor_scalar(xn_all[:, n, :], x_res[:, n, :], ln_mv[:, n, 0:1], ln_rstd[:, n:n + 1],
                                             ALU.subtract, ALU.mult)
                last.then_inc(ln_pre.xn, 1)

            pre_stats(0)
            pre_stats(1)
            pre_apply(0)
            eng.wait_ge(cast_ready, 2)
            minus_ones(eng, 0)
            pre_apply(1)
            minus_ones(eng, 1)
            eng.wait_ge(const_ready, 3)
            eng.tensor_scalar(neg_mask_eye[:, :], ident[:, :], -MASK_A, None, ALU.mult).then_inc(cast_ready, 1)
            eng.tensor_copy(ident_bf[:, :], ident[:, :])
            for l in range(2):
                eng.wait_ge(bo_ps, l + 1)
                eng.wait_ge(bias_loaded, 8 * DMA)
                eng.tensor_tensor(bo[l][:, :], ps[:, BANK_T[l], 0:D], bo[l][:, :], ALU.add).then_inc(bo_new, 1)
            eng.wait_ge(ffn_loaded, 5 * DMA)
            for w in range(2):
                eng.tensor_reduce(wq_stat[:, w:w + 1], ffn_raw[:, w, :, :], AX.XY, ALU.add,
                                  apply_absolute_value=True).then_inc(f_stat, 1)
            eng.wait_ge(f_mean, 1)
            eng.tensor_scalar(wq_stat[:, 2:4], ps[:, BANK_T[2], 0:2], QUANT_EPS, None, ALU.max).then_inc(f_tern, 1)
            eng.wait_ge(f_tern, 1)
            eng.reciprocal(wq_stat[:, 6:8], wq_stat[:, 2:4]).then_inc(f_tern, 1)
            eng.wait_ge(f_tern, 2)
            for w in range(2):
                eng.tensor_scalar(ffn_raw[:, w, :, :], ffn_raw[:, w, :, :], wq_stat[:, 6 + w:7 + w], ROUND,
                                  ALU.mult, ALU.add).then_inc(f_tern, 1)
            eng.wait_ge(f_tern, 4)
            for w in range(2):
                eng.tensor_scalar(ffn_raw[:, w, :, :], ffn_raw[:, w, :, :], ROUND, 1.0, ALU.subtract,
                                  ALU.min).then_inc(f_tern, 1)
            eng.wait_ge(f_tern, 6)
            eng.tensor_scalar(ffn_raw[:, :, :, :], ffn_raw[:, :, :, :], -1.0, None, ALU.max).then_inc(f_tern, 1)
            eng.tensor_scalar(conv_w[:, :, :], conv_w[:, :, :], wq_stat[:, 2:3], None, ALU.mult).then_inc(f_tern, 1)
            attention_vector(eng, 0)
            if stages >= 2:
                ffn_vector(eng)
            if stages >= 3:
                attention_vector(eng, 1)
            if stages >= 4:
                for e in range(E):
                    for w, (hi, lo) in enumerate(((fc1_hi, fc1_lo), (fc2_hi, fc2_lo))):
                        eng.wait_ge(fc_hi, 2 * e + w + 1)
                        eng.tensor_tensor(lo[:, e, :, :], ps[:, e % 3 * 2 + w, :].rearrange("p (c h) -> p c h", c=EC),
                                          hi[:, e, :, :].bitcast(F32), ALU.subtract).then_inc(fc_done, 1)
                eng.tensor_tensor(pick[:, :], ident[:, 0:E], ident[:, E:2 * E], ALU.add).then_inc(w_split, 1)
                routing(eng)
                eng.tensor_copy(w_parts[:, :, 0, :], w_te[:, :, :]).then_inc(w_split, 1)
                eng.wait_ge(w_split, 2)
                eng.tensor_tensor(w_parts[:, :, 1, :], w_te[:, :, :], w_parts[:, :, 0, :].bitcast(F32),
                                  ALU.subtract).then_inc(w_split, 1)

                def scale(g, e, c):
                    k = (g * E + e) * EC + c
                    eng.wait_ge(h_silu, k + 1)
                    eng.wait_ge(w_ps, g * E + e + 1)
                    if e > 0 or after(g, 0):
                        if c == EC - 1:
                            eng.wait_ge(h_lo_last, g * E + e)
                        else:
                            eng.wait_ge(h_lo, (g * E + e - 1) * (EC - 1) + c + 1)
                    eng.tensor_tensor(h_scaled_sb[:, c, :], h_act_sb[:, c, :], ps[:, 4 + e % 2, :],
                                      ALU.mult).then_inc(h_scaled, 1)

                def low(g, e, c):
                    u = g * E + e
                    eng.wait_ge(h_hi, u * EC + c + 1)
                    if e > 0 or after(g, 0):
                        eng.wait_ge(h_used, (u - 1) * EC + c + 1)
                    eng.tensor_tensor(h_lo_sb[:, c, :], h_scaled_sb[:, c, :], h_hi_sb[:, c, :].bitcast(F32),
                                      ALU.subtract).then_inc(h_lo, 1)

                def group(g):
                    for e in range(E):
                        for c in range(EC):
                            scale(g, e, c)
                            if c > 0:
                                low(g, e, c - 1)
                        if e == 1 and after(g, 0):
                            add_group(g - 1)

                def add_group(g):
                    eng.wait_ge(yT_ps, g + 1)
                    x_group = x_res[:, bass.ds(g * GT, GT), :]
                    eng.tensor_tensor(x_group, ps[:, 7, :].rearrange("p (i d) -> p i d", i=GT), x_group,
                                      ALU.add).then_inc(y_used, 1)

                group(0)
                with eng.Fori(1, NG) as g:
                    group(g)
                add_group(NG - 1)

        def attention_tensor(eng, l, after_first=None):
            a, at = att[l], AT[l]
            s = (ln_a0, ln_a1)[l]
            src_ln = (ln_pre, ln_f0)[l]
            M = BANK_M

            def body(b, r):
                for n in range(H):
                    if exists(b + 1):
                        scores(b + 1, 1 - r, n)
                    if n % HPS == at["pv"] % HPS:
                        if n == at["pv"] % HPS:
                            if exists(b - 1):
                                weighted_v(b - 1, 1 - r, 3)
                        elif exists(b):
                            weighted_v(b, r, (n - at["pv"]) // HPS)
                    if exists(b):
                        shifted(b, r, n)
                    extras(b, r, n)

            def scores(b, r, n):
                st, j = n // HPS, n % HPS
                if n % 8 == 0:
                    eng.wait_ge(a.stack[n // 8], (b + 1) * 5 * DMA)
                if n >= 2 or after(b, 0):
                    eng.wait_ge(a.s_max, b * 16 + n - 1)
                bank = BANK_S[n % 2]
                for i in range(NT):
                    mm = eng.matmul(ps[:, bank, i * S:(i + 1) * S], q_stack[r][:, st, i * P:(i + 1) * P],
                                    k_blocks[r][:, st, j, :], start=True, stop=True)
                mm.then_inc(a.s_ps, 1)

            def shifted(b, r, n):
                st, j = n // HPS, n % HPS
                if n % 8 == 0:
                    eng.wait_ge(a.m_in[n // 8], (b + 1) * 2 * DMA)
                if l == 1 and n == 0:
                    eng.wait_ge(a.kT_sb, b + 1)
                back = 3 if n >= 3 else (1, 3, 2)[n]
                if n >= 3 or after(b, 0):
                    eng.wait_ge(a.p_sb, b * 16 + n - back + 1)
                bank = BANK_T[n % 3]
                if l == 1:
                    eng.matmul(ps[:, bank, :], neg_mask_eye[:, :], mask_k[r][:, :, :].rearrange("p i k -> p (i k)"),
                               start=True, stop=False)
                for k in range(NT):
                    mm = eng.matmul(ps[:, bank, k * S:(k + 1) * S], k_blocks[r][:, st, j, k * P:(k + 1) * P],
                                    q_stack[r][:, st, :], start=(l == 0), stop=(l == 0 or k == NT - 1))
                mm.then_inc(a.t_ps, 1)

            def weighted_v(b, r, st):
                eng.wait_ge(a.p_sb, b * 16 + st * HPS + HPS)
                if st == 0:
                    eng.wait_ge(a.v_sb, b + 1)
                    if after(b, 0):
                        eng.wait_ge(a.o_norm, b * 2)
                    else:
                        eng.wait_ge(a.mT_sb, 2)
                if st == 2 and (after(b, 0)):
                    eng.wait_ge(a.x_new, b)
                bank = BANK_O[st // 2]
                col = st % 2 * S
                for k in range(NT):
                    for j in range(HPS):
                        mm = eng.matmul(ps[j * HR:(j + 1) * HR, bank, col:col + S], v_aug[r][:, k, st * HPS + j, :],
                                        probs[:, st % 2, j, k, :], start=(k == 0), stop=(k == NT - 1),
                                        tile_position=(0, j * HR))
                mm.then_inc(a.pv, 1)

            def max_transposes(b, half):
                bank = (M, BANK_O[0])[half]
                eng.wait_ge(a.m_split, b * 2 + half + 1)
                for st in range(2):
                    for i in range(NT):
                        mm = eng.transpose(ps[0:2 * HPS, bank, st * S + i * P:st * S + (i + 1) * P],
                                           max_split[:, i, half, st, :, :].bitcast(F32).rearrange("p m j -> p (m j)"),
                                           ident[:, :])
                mm.then_inc(a.mT_ps, 1)

            def extras(b, r, n):
                if n == at["ctx"] and exists(b + 2):
                    eng.wait_ge(a.ctx_in, (b + 3) * DMA)
                    if exists(b - 2):
                        eng.wait_ge(*((s.xs, b - 1) if l == 0 else (a.r_log, b - 1)))
                    elif exists(b):
                        eng.wait_ge(a.mT_sb, b * 2 + 1)
                    elif exists(b + 1):
                        eng.wait_ge(a.qk_sum, 1)
                    for i in range(NT):
                        mm = eng.transpose(ps[:, M, i * P:(i + 1) * P], ctx_in[:, i, :], ident[:, :])
                    mm.then_inc(a.cT_ps, 1)
                if n == at["max1"] and exists(b):
                    if after(b, 0):
                        eng.wait_ge(a.o_sb, b * 2 - 1)
                    max_transposes(b, 1)
                if n == at["qk"] and exists(b + 2):
                    eng.wait_ge(a.cT_sb, b + 3)
                    if l == 0:
                        eng.wait_ge(src_ln.xs, NB // 2 if after(b, -2) else NB // 4)
                    elif not after(b, -2):
                        eng.wait_ge(src_ln.xs, NB)
                    xT = xnT_all[:, bass.ds(b + 2, 1), :].rearrange("p o t -> p (o t)")
                    eng.matmul(ps[:, M, 0:S], wq[l][:, :], xT, start=True, stop=True)
                    eng.matmul(ps[:, M, S:2 * S], wk[l][:, :], ctxT[r][:, :], start=True, stop=True).then_inc(a.qk_ps, 1)
                if n == at["v"] and exists(b + 1):
                    if exists(b + 2):
                        eng.wait_ge(a.qk_sum, b + 3)
                    else:
                        eng.wait_ge(*((s.xs, b - 1) if l == 0 else (a.r_log, b - 1)))
                    for i in range(NT):
                        mm = eng.matmul(ps[:, M, i * D:(i + 1) * D], ctxT[1 - r][:, i * P:(i + 1) * P], wv[l][:, :],
                                        start=True, stop=True)
                    mm.then_inc(a.v_ps, 1)
                if l == 1 and n == at["mask"] and exists(b + 1):
                    eng.wait_ge(a.k_q, b + 2)
                    eng.wait_ge(a.v_sb, b + 2)
                    for k in range(NT):
                        for i in range(NT):
                            mm = eng.transpose(ps[:, M, k * S + i * P:k * S + (i + 1) * P],
                                               mask_q[1 - r][:, i, k * P:(k + 1) * P], ident[:, :])
                    mm.then_inc(a.kT_ps, 1)
                if n == at["max0"] and exists(b + 1):
                    eng.wait_ge(*((a.v_sb, b + 2) if l == 0 else (a.kT_sb, b + 2)))
                    max_transposes(b + 1, 0)
                if n == at["x"] and exists(b - 1):
                    if exists(b + 1):
                        eng.wait_ge(a.mT_sb, b * 2 + 3)
                    elif exists(b - 2):
                        eng.wait_ge(*((s.xs, b - 1) if l == 0 else (a.r_log, b - 1)))
                    xn_transposes(eng, s, b - 1, M, 0, (s.q, b * 5) if l == 0 else (s.xn, b))
                if l == 1 and n == 15 and exists(b - 1):
                    eng.wait_ge(a.r_x, b)
                    eng.wait_ge(a.x_hi, b)
                    for i in range(NT):
                        mm = eng.matmul(ps[:, M, i * E:(i + 1) * E], r_x[:, i * P:(i + 1) * P], routerT[:, :],
                                        start=True, stop=True)
                    mm.then_inc(a.r_ps, 1)
                output_steps(b, n)

            def output_steps(b, n):
                if not exists(b - 1):
                    return
                if n == at["outT"]:
                    eng.wait_ge(a.o_sb, b * 2)
                    if exists(b):
                        eng.wait_ge(a.mT_sb, b * 2 + 2)
                    for i in range(NT):
                        for st in range(SETS):
                            mm = eng.transpose(ps[:, BANK_O[1 - i], st * P:(st + 1) * P], o_raw[:, st, i * P:(i + 1) * P],
                                               ident[:, :])
                        mm.then_inc(a.oT_ps, 1)
                if n == at["normT"]:
                    eng.wait_ge(a.o_norm, b * 2)
                    for i in range(NT):
                        mm = eng.transpose(ps[:, BANK_O[1], i * P:(i + 1) * P], o_norm[:, i, :], ident[:, :])
                    mm.then_inc(a.nT_ps, 1)
                if n == at["y"]:
                    eng.wait_ge(a.nT_sb, b)
                    for i in range(NT):
                        mm = eng.matmul(ps[:, BANK_O[1], S + i * D:S + (i + 1) * D], o_normT[:, i * P:(i + 1) * P],
                                        wo[l][:, :], start=True, stop=True)
                    mm.then_inc(a.y_ps, 1)

            bodies(eng, body, after_first)

        def ffn_tensor(eng):
            def hidden(b, r):
                if after(b, 1):
                    eng.wait_ge(h_conv, (b - 1) * 2 * FC)
                for c in range(FC):
                    mm = eng.matmul(hidden_ps(r, c), w1T[:, c, :], one(xnT_all, b), start=True, stop=True)
                    if c % 2 == 1:
                        mm.then_inc(h_ps, 1)

            def act_transposes(b):
                eng.wait_ge(h_act, b + 1)
                for i in range(NT):
                    eng.wait_ge(g_round, b * NT)
                    for c in range(FC):
                        mm = eng.transpose(ps[:, 4 + i, c * P:(c + 1) * P], f_act[:, c, i * P:(i + 1) * P], ident[:, :])
                    mm.then_inc(g_ps, 1)

            def int_transposes(b):
                for i in range(NT):
                    eng.wait_ge(g_int, b * 2 * NT + NT + i + 1)
                    eng.wait_ge(gi_sb, b * NT + i)
                    bank = ps[:, 6, i * 256:(i + 1) * 256].bitcast(BF16)
                    for c in range(FC):
                        mm = eng.transpose(bank[:, c * P:(c + 1) * P], f_int[:, i, c * P:(c + 1) * P], ident_bf[:, :])
                    mm.then_inc(gi_ps, 1)

            def output(b):
                eng.wait_ge(gi_sb, b * NT + NT)
                eng.wait_ge(ln_f0.xs, b)
                for i in range(NT):
                    for c in range(FC):
                        mm = eng.matmul(ps[:, 7, i * P:(i + 1) * P], f_intT[:, i, c, :], w2T[:, c, :],
                                        start=(c == 0), stop=(c == FC - 1))
                mm.then_inc(fy_ps, 1)

            def tokens(b):
                xn_transposes(eng, ln_f0, b, 7, S, (ln_f0.xn, b + 1))

            hidden(0, 0)

            def step(b, r):
                if exists(b - 1):
                    int_transposes(b - 1)
                if exists(b - 2):
                    tokens(b - 2)
                if exists(b + 2):
                    hidden(b + 2, r)
                if exists(b - 1):
                    output(b - 1)
                if exists(b + 1):
                    act_transposes(b + 1)

            ffn_steps(eng, step)
            tokens(NB - 1)

        @block.tensor
        def _(eng):
            eng.wait_ge(const_ready, 3)
            eng.wait_ge(w_loaded, 4 * DMA)
            for n in range(4):
                mm = eng.transpose(ps[:, BANK_M, n * D:(n + 1) * D], w_raw[:, n, :], ident[:, :])
            mm.then_inc(wT_ps, 1)

            def pre_transposes(half):
                eng.wait_ge(ln_pre.xn, half + 1)
                for g in range(half * NB // 4, (half + 1) * NB // 4):
                    for i in range(2 * NT):
                        mm = eng.transpose(ps[:, g, i * P:(i + 1) * P], xn_all[:, 2 * g * NT + i, :], ident[:, :])
                    mm.then_inc(ln_pre.xT, 1)

            pre_transposes(0)
            eng.wait_ge(wT_sb, 1)

            def small_products():
                pre_transposes(1)
                eng.wait_ge(bias_ready, 4)
                eng.wait_ge(w1_loaded, 4 * DMA)
                eng.wait_ge(ln_pre.xs, NB // 2)
                for l in range(2):
                    eng.matmul(ps[:, BANK_T[l], 0:D], bv_wide[:, l, :], wo[l][:, :], start=True, stop=True).then_inc(bo_ps, 1)
                eng.wait_ge(const_ready, 8)
                eng.wait_ge(f_stat, 2)
                eng.matmul(ps[:, BANK_T[2], 0:2], mean_ones[:, :], wq_stat[:, 0:2], start=True, stop=True).then_inc(f_mean, 1)

            attention_tensor(eng, 0, small_products)
            if stages >= 2:
                eng.wait_ge(f_tern, 7)
                eng.wait_ge(att[0].s_max, NB * 16)
                for w in range(2):
                    for c in range(FC):
                        mm = eng.transpose(ps[:, w, c * P:(c + 1) * P], ffn_raw[:, w, c, :], ident[:, :])
                    mm.then_inc(wT_ps, 1)
                eng.transpose(ps[:, 2, 0:E], router_raw[:, :], ident[0:E, 0:E]).then_inc(wT_ps, 1)
                eng.wait_ge(wT_sb, 5)
                eng.wait_ge(att[0].p_sb, NB * 16)
                eng.wait_ge(att[0].x_new, NB)
                eng.wait_ge(ln_a0.xs, NB)
                ffn_tensor(eng)
            if stages >= 3:
                eng.wait_ge(ln_f0.xs, NB)
                attention_tensor(eng, 1)
            if stages >= 4:
                eng.wait_ge(att[1].x_new, NB)
                for e in range(E):
                    eng.wait_ge(fc_loaded[e % 2], (e // 2 + 1) * 2 * DMA)
                    if e >= 3:
                        eng.wait_ge(fc_done, 2 * (e - 2))
                    for w in range(2):
                        for c in range(EC):
                            mm = eng.transpose(ps[:, e % 3 * 2 + w, c * P:(c + 1) * P],
                                               fc_raw[:, e % 2, w, c * P:(c + 1) * P], ident[:, :])
                        mm.then_inc(fc_ps, 1)
                eng.wait_ge(att[1].x_lo, NB)
                eng.wait_ge(att[1].r_log, NB)
                eng.wait_ge(fc_done, 2 * E)
                eng.wait_ge(w_split, 3)
                for g in range(NG):
                    for i in range(GT):
                        mm = eng.transpose(ps[0:2 * E, 4 + g, i * P:(i + 1) * P],
                                           w_parts[:, g * GT + i, :, :].bitcast(F32).rearrange("p m e -> p (m e)"),
                                           ident[:, :])
                    mm.then_inc(wT_in_ps, 1)
                eng.wait_ge(wT_ready, NG)

                def up(g, e, c):
                    if e > 0 or after(g, 0):
                        eng.wait_ge(h_silu, (g * E + e - 1) * EC + c + 1)
                    xh = xhT_all[:, :, :].rearrange("p b t -> p (b t)")[:, bass.ds(g * GTP, GTP)]
                    xl = xlT_all[:, :, :].rearrange("p b t -> p (b t)")[:, bass.ds(g * GTP, GTP)]
                    eng.matmul(ps[:, c, :], fc1_hi[:, e, c, :], xh, start=True, stop=False)
                    eng.matmul(ps[:, c, :], fc1_hi[:, e, c, :], xl, start=False, stop=False)
                    eng.matmul(ps[:, c, :], fc1_lo[:, e, c, :], xh, start=False, stop=True).then_inc(fc1_ps, 1)

                def weight_rows(g, e):
                    if e > 1 or after(g, 0):
                        eng.wait_ge(h_scaled, (g * E + e - 1) * EC)
                    rows = wT[:, bass.ds(g * GT, GT), :].rearrange("p i t -> p (i t)")
                    eng.matmul(ps[:, 4 + e % 2, :], pick[:, e:e + 1].to_broadcast([P, P]), rows,
                               start=True, stop=True).then_inc(w_ps, 1)

                def down(g, e, c):
                    u = g * E + e
                    if c == EC - 1:
                        eng.wait_ge(h_lo_last, u + 1)
                    else:
                        eng.wait_ge(h_lo, u * (EC - 1) + c + 1)
                    if e == 0 and c == 0 and after(g, 0):
                        eng.wait_ge(y_sb, g)
                    first, last = e == 0 and c == 0, e == E - 1 and c == EC - 1
                    eng.matmul(ps[:, 6, :], fc2_hi[:, e, c, :], h_hi_sb[:, c, :], start=first, stop=False)
                    eng.matmul(ps[:, 6, :], fc2_lo[:, e, c, :], h_hi_sb[:, c, :], start=False, stop=False)
                    mm = eng.matmul(ps[:, 6, :], fc2_hi[:, e, c, :], h_lo_sb[:, c, :], start=False, stop=last)
                    mm.then_inc(h_used, 1)

                def group(g):
                    for e in range(E):
                        for c in range(EC):
                            up(g, e, c)
                            if c == 0:
                                weight_rows(g, e)
                            if e > 0:
                                down(g, e - 1, c)
                            elif after(g, 0):
                                down(g - 1, E - 1, c)
                        if e == 1 and after(g, 0):
                            output(g - 1)

                def output(g):
                    eng.wait_ge(y_sb, g + 1)
                    if after(g, 0):
                        eng.wait_ge(y_used, g)
                    for i in range(GT):
                        mm = eng.transpose(ps[:, 7, i * P:(i + 1) * P], yT[:, i * P:(i + 1) * P], ident[:, :])
                    mm.then_inc(yT_ps, 1)

                group(0)
                with eng.Fori(1, NG) as g:
                    group(g)
                for c in range(EC):
                    down(NG - 1, E - 1, c)
                output(NG - 1)


_INPUTS = (
    ["x", "ctx_1024", "mask_Bx1xSxS2_ik1"]
    + [f"L0_xattn_{n}" for n in ("Wq", "bq", "Wk", "bk", "Wv", "bv", "Wo", "bo")]
    + ["L0_ffn_w1", "L0_ffn_conv_w", "L0_ffn_conv_b", "L0_ffn_w2"]
    + [f"L1_xattn_{n}" for n in ("Wq", "bq", "Wk", "bk", "Wv", "bv", "Wo", "bo")]
    + ["L1_ffn_router_w", "L1_ffn_fc1_w", "L1_ffn_fc2_w"]
)


def kernel(**inputs):
    import concourse.bacc as bacc
    from concourse.bass_utils import run_bass_kernel_spmd

    nc = bacc.Bacc("TRN2", target_bir_lowering=False, num_devices=1)
    arrays, aps = {}, {}
    for name in _INPUTS:
        a = np.ascontiguousarray(inputs[name])
        arrays[name] = a
        aps[name] = nc.dram_tensor(name, a.shape, mybir.dt.from_np(a.dtype), kind="ExternalInput").ap()
    out = nc.dram_tensor("out", inputs["x"].shape, F32, kind="ExternalOutput").ap()
    build(nc, aps, out)
    r = run_bass_kernel_spmd(nc, [arrays], core_ids=[0])
    return r.results[0]["out"]
```
